# Optimizing a Trainium2 kernel written in Bass

```python
import numpy as np
import jax
import jax.numpy as jnp

def _softmax(x, axis=-1):
    return jax.nn.softmax(x, axis=axis)

def _gelu(x):
    return jax.nn.gelu(x, approximate=True)

def _silu(x):
    return jax.nn.silu(x)

def _sigmoid(x):
    return jax.nn.sigmoid(x)

def _layernorm(x, axis=-1, eps=1e-05):
    m = jnp.mean(x, axis=axis, keepdims=True)
    v = jnp.var(x, axis=axis, keepdims=True)
    return (x - m) / jnp.sqrt(v + eps)

def _scatter_add(tgt, idx, src, axis=0):
    return tgt.at[idx].add(src)

def _segment_sum(src, seg, n):
    return jax.ops.segment_sum(src, seg, n)
kernel_name = 'mk_seq_postln_d1_jaxref_r8_4600a5'

def setup_inputs(seed: int=0):
    np.random.seed(seed)
    _w = jnp.asarray

    def _L0_attn_setup():
        import jax, jax.numpy as jnp
        import numpy as np
        DIM = 256
        N_HEAD = 16
        N_KV_HEAD = 4
        DQK = 128
        DV = DIM // N_HEAD
        N_REP = N_HEAD // N_KV_HEAD
        WIN = 64
        FRONT = 32
        SEQ = 512
        THETA = 10000.0

        def rope_cos_sin(seq_len, dim, theta=THETA):
            inv_freq = 1.0 / theta ** (np.arange(0, dim, 2)[:dim // 2].astype(np.float32) / dim)
            t = np.arange(seq_len, dtype=np.float32)
            ang = np.outer(t, inv_freq)
            return (jnp.asarray(np.cos(ang)), jnp.asarray(np.sin(ang)))

        def apply_rope(x, cos, sin):
            xr = x[..., 0::2]
            xi = x[..., 1::2]
            c = cos[None, :, None, :]
            s = sin[None, :, None, :]
            out_r = xr * c - xi * s
            out_i = xr * s + xi * c
            return jnp.stack([out_r, out_i], axis=-1).reshape(x.shape)

        def build_mask(seq_len, window, front):
            i = jnp.arange(seq_len)[:, None]
            j = jnp.arange(seq_len)[None, :]
            band = (j <= i) & (j > i - window)
            front_ok = (j < front) & (j <= i - window)
            allowed = band | front_ok
            return jnp.where(allowed, 0.0, -jnp.inf).astype(jnp.float32)
        key = jax.random.key(seed)
        ks = jax.random.split(key, 5)
        B = 1
        scale_in = 1.0 / np.sqrt(DIM)
        x = jax.random.normal(ks[0], (B, SEQ, DIM), dtype=jnp.float32)
        wq = jax.random.normal(ks[1], (DIM, N_HEAD * DQK), dtype=jnp.float32) * scale_in
        wk = jax.random.normal(ks[2], (DIM, N_KV_HEAD * DQK), dtype=jnp.float32) * scale_in
        wv = jax.random.normal(ks[3], (DIM, N_KV_HEAD * DV), dtype=jnp.float32) * scale_in
        wo = jax.random.normal(ks[4], (N_HEAD * DV, DIM), dtype=jnp.float32) * scale_in
        return {'x': x, 'wq': wq, 'wk': wk, 'wv': wv, 'wo': wo}
    _L0_attn_in = _L0_attn_setup()

    def _L0_ffn_setup():
        import jax, jax.numpy as jnp
        import numpy as np
        EPS = 1e-06
        K_STEPS = 4
        USE_GATING = True

        def layer_norm(x, gamma, beta):
            mu = jnp.mean(x, axis=-1, keepdims=True)
            var = jnp.mean(jnp.square(x - mu), axis=-1, keepdims=True)
            return (x - mu) * jax.lax.rsqrt(var + EPS) * gamma + beta
        key = jax.random.key(seed)
        B, L, D, H = (4, 512, 256, 1024)
        ks = jax.random.split(key, 16)
        s = 0.02
        return {'x': jax.random.normal(ks[0], (B, L, D), dtype=jnp.float32), 'in_gamma': jnp.ones((D,), jnp.float32), 'in_beta': jnp.zeros((D,), jnp.float32), 'agg_w': jax.random.normal(ks[1], (D, D), jnp.float32) * s, 'agg_b': jnp.zeros((D,), jnp.float32), 'pn_gamma': jnp.ones((D,), jnp.float32), 'pn_beta': jnp.zeros((D,), jnp.float32), 'd1_w': jax.random.normal(ks[2], (D, H), jnp.float32) * s, 'd1_b': jnp.zeros((H,), jnp.float32), 'd2_w': jax.random.normal(ks[3], (H, D), jnp.float32) * s, 'd2_b': jnp.zeros((D,), jnp.float32), 'bc_w': jax.random.normal(ks[4], (D, D), jnp.float32) * s, 'bc_b': jnp.zeros((D,), jnp.float32), 'gate_w': jax.random.normal(ks[5], (D, D), jnp.float32) * s, 'gate_b': jnp.zeros((D,), jnp.float32), 'out_gamma': jnp.ones((D,), jnp.float32), 'out_beta': jnp.zeros((D,), jnp.float32)}
    _L0_ffn_in = _L0_ffn_setup()
    _d = {'L0_attn_x': _L0_attn_in['x'], 'L0_attn_wq': _L0_attn_in['wq'], 'L0_attn_wk': _L0_attn_in['wk'], 'L0_attn_wv': _L0_attn_in['wv'], 'L0_attn_wo': _L0_attn_in['wo'], 'L0_ffn_in_gamma': _L0_ffn_in['in_gamma'], 'L0_ffn_in_beta': _L0_ffn_in['in_beta'], 'L0_ffn_agg_w': _L0_ffn_in['agg_w'], 'L0_ffn_agg_b': _L0_ffn_in['agg_b'], 'L0_ffn_pn_gamma': _L0_ffn_in['pn_gamma'], 'L0_ffn_pn_beta': _L0_ffn_in['pn_beta'], 'L0_ffn_d1_w': _L0_ffn_in['d1_w'], 'L0_ffn_d1_b': _L0_ffn_in['d1_b'], 'L0_ffn_d2_w': _L0_ffn_in['d2_w'], 'L0_ffn_d2_b': _L0_ffn_in['d2_b'], 'L0_ffn_bc_w': _L0_ffn_in['bc_w'], 'L0_ffn_bc_b': _L0_ffn_in['bc_b'], 'L0_ffn_gate_w': _L0_ffn_in['gate_w'], 'L0_ffn_gate_b': _L0_ffn_in['gate_b'], 'L0_ffn_out_gamma': _L0_ffn_in['out_gamma'], 'L0_ffn_out_beta': _L0_ffn_in['out_beta']}
    _x0 = _d['L0_attn_x']
    _d['L0_attn_x'] = jax.random.normal(jax.random.fold_in(jax.random.key(seed), 1), (4, 1024, 256), dtype=_x0.dtype)
    del _x0
    return _d

def reference(L0_attn_x, L0_attn_wq, L0_attn_wk, L0_attn_wv, L0_attn_wo, L0_ffn_in_gamma, L0_ffn_in_beta, L0_ffn_agg_w, L0_ffn_agg_b, L0_ffn_pn_gamma, L0_ffn_pn_beta, L0_ffn_d1_w, L0_ffn_d1_b, L0_ffn_d2_w, L0_ffn_d2_b, L0_ffn_bc_w, L0_ffn_bc_b, L0_ffn_gate_w, L0_ffn_gate_b, L0_ffn_out_gamma, L0_ffn_out_beta):

    def _L0_attn_ref(x, wq, wk, wv, wo):
        import jax, jax.numpy as jnp
        import numpy as np
        DIM = 256
        N_HEAD = 16
        N_KV_HEAD = 4
        DQK = 128
        DV = DIM // N_HEAD
        N_REP = N_HEAD // N_KV_HEAD
        WIN = 64
        FRONT = 32
        SEQ = 512
        THETA = 10000.0

        def rope_cos_sin(seq_len, dim, theta=THETA):
            inv_freq = 1.0 / theta ** (np.arange(0, dim, 2)[:dim // 2].astype(np.float32) / dim)
            t = np.arange(seq_len, dtype=np.float32)
            ang = np.outer(t, inv_freq)
            return (jnp.asarray(np.cos(ang)), jnp.asarray(np.sin(ang)))

        def apply_rope(x, cos, sin):
            xr = x[..., 0::2]
            xi = x[..., 1::2]
            c = cos[None, :, None, :]
            s = sin[None, :, None, :]
            out_r = xr * c - xi * s
            out_i = xr * s + xi * c
            return jnp.stack([out_r, out_i], axis=-1).reshape(x.shape)

        def build_mask(seq_len, window, front):
            i = jnp.arange(seq_len)[:, None]
            j = jnp.arange(seq_len)[None, :]
            band = (j <= i) & (j > i - window)
            front_ok = (j < front) & (j <= i - window)
            allowed = band | front_ok
            return jnp.where(allowed, 0.0, -jnp.inf).astype(jnp.float32)
        B, S, _ = x.shape
        q = (x @ wq).reshape(B, S, N_HEAD, DQK)
        k = (x @ wk).reshape(B, S, N_KV_HEAD, DQK)
        v = (x @ wv).reshape(B, S, N_KV_HEAD, DV)
        cos, sin = rope_cos_sin(S, DQK)
        q = apply_rope(q, cos, sin)
        k = apply_rope(k, cos, sin)
        q = q.transpose(0, 2, 1, 3)
        k = k.transpose(0, 2, 1, 3)
        v = v.transpose(0, 2, 1, 3)
        k = jnp.repeat(k, N_REP, axis=1)
        v = jnp.repeat(v, N_REP, axis=1)
        mask = build_mask(S, WIN, FRONT)
        scores = jnp.einsum('bhqd,bhkd->bhqk', q, k) / np.sqrt(DQK).astype(np.float32)
        scores = scores + mask[None, None, :, :]
        attn = jax.nn.softmax(scores, axis=-1)
        out = jnp.einsum('bhqk,bhkd->bhqd', attn, v)
        out = out.transpose(0, 2, 1, 3).reshape(B, S, N_HEAD * DV)
        return out @ wo

    def _L0_ffn_ref(x, in_gamma, in_beta, agg_w, agg_b, pn_gamma, pn_beta, d1_w, d1_b, d2_w, d2_b, bc_w, bc_b, gate_w, gate_b, out_gamma, out_beta):
        import jax, jax.numpy as jnp
        import numpy as np
        EPS = 1e-06
        K_STEPS = 4
        USE_GATING = True

        def layer_norm(x, gamma, beta):
            mu = jnp.mean(x, axis=-1, keepdims=True)
            var = jnp.mean(jnp.square(x - mu), axis=-1, keepdims=True)
            return (x - mu) * jax.lax.rsqrt(var + EPS) * gamma + beta
        x_norm = layer_norm(x, in_gamma, in_beta)
        thought = x_norm[:, -1, :] @ agg_w + agg_b
        for _ in range(K_STEPS):
            t = layer_norm(thought, pn_gamma, pn_beta)
            t = jax.nn.gelu(t @ d1_w + d1_b, approximate=False)
            thought = thought + (t @ d2_w + d2_b)
        broadcast = (thought @ bc_w + bc_b)[:, None, :]
        if USE_GATING:
            gate = jax.nn.sigmoid(x @ gate_w + gate_b)
            out = x + gate * broadcast
        else:
            out = x + broadcast
        return layer_norm(out, out_gamma, out_beta)
    x = L0_attn_x
    x = _layernorm(x + _L0_attn_ref(x, L0_attn_wq, L0_attn_wk, L0_attn_wv, L0_attn_wo), axis=-1)
    x = _layernorm(x + _L0_ffn_ref(x, L0_ffn_in_gamma, L0_ffn_in_beta, L0_ffn_agg_w, L0_ffn_agg_b, L0_ffn_pn_gamma, L0_ffn_pn_beta, L0_ffn_d1_w, L0_ffn_d1_b, L0_ffn_d2_w, L0_ffn_d2_b, L0_ffn_bc_w, L0_ffn_bc_b, L0_ffn_gate_w, L0_ffn_gate_b, L0_ffn_out_gamma, L0_ffn_out_beta), axis=-1)
    return x

_drawn_inputs = setup_inputs


def setup_inputs(seed=0):
    import zlib

    import numpy as np

    out = dict(_drawn_inputs(seed))
    spreads = {'L0_ffn_in_gamma': (1.0, 0.6),
     'L0_ffn_in_beta': (0.0, 0.8),
     'L0_ffn_agg_b': (0.0, 0.598),
     'L0_ffn_pn_gamma': (1.0, 0.6),
     'L0_ffn_pn_beta': (0.0, 0.8),
     'L0_ffn_d1_b': (0.0, 0.716),
     'L0_ffn_d2_b': (0.0, 0.1),
     'L0_ffn_bc_b': (0.0, 0.328),
     'L0_ffn_gate_b': (0.0, 0.8),
     'L0_ffn_out_gamma': (1.0, 0.2),
     'L0_ffn_out_beta': (0.0, 0.1)}
    factors = {'L0_ffn_gate_w': 6.027}
    for name, (base, spread) in spreads.items():
        noise = np.random.default_rng([zlib.crc32(name.encode()), seed]).standard_normal(out[name].shape)
        drawn = base * np.exp(spread * noise) if base else spread * noise
        out[name] = jnp.asarray(drawn.astype(out[name].dtype))
    for name, factor in factors.items():
        out[name] = (out[name] * factor).astype(out[name].dtype)
    return out
```

```python
from contextlib import ExitStack

import concourse.bass as bass
from concourse import mybir
from concourse.alu_op_type import AluOpType as ALU

P = 128
D = 256
KT = D // P
SEQ, BATCH = 1024, 4
CHUNK = 512
NCH = SEQ * BATCH // CHUNK
NSTORE = BATCH
TILES = CHUNK // P
HEADS, GROUPS, REP = 16, 4, 4
DV = D // HEADS
VW = DV + 1
BLK, FRONT = 64, 32
NBLK = CHUNK // BLK
EXT = BLK + FRONT
KSPLIT = EXT + 3 * BLK
XW = EXT + CHUNK
KEYS = FRONT + 2 * BLK
H = 1024
HT = H // P
STEPS = 4
WQ0, WK0, WV0 = 0, HEADS * P, (HEADS + GROUPS) * P
WALL = WV0 + GROUPS * DV
EPS1, EPS2 = 1e-5, 1e-6

EPILOGUE = {(2, "A"): ["OT0"], (2, "B"): ["OT1"], (3, "A"): ["OP0"], (3, "B"): ["OP1"], (3, "C"): ["BN"],
            (4, "B"): ["NM"], (5, "A"): ["X1T0"], (5, "B"): ["X1T1"], (6, "A"): ["G0"], (6, "B"): ["G1"]}
PREPARE = {(11, "B"): ["XT0"], (12, "A"): ["XT1"], (12, "B"): ["XTE"]}
THOUGHT = ["TN", "TA"] + ["TT", "TH", "TD"] * STEPS + ["TU", "TB", "TC0", "TC1"]
PE_FED = ("OT0", "OT1", "X1T0", "X1T1", "XT0", "XT1", "XTE")
FINAL = ["FA", "FB", "FC", "FD", "FE"]
MISC_JOBS = {"V", "OT0", "OT1", "OP0", "OP1", "X1T0", "X1T1", "G0", "G1", "XT0", "XT1", "XTE"} | set(THOUGHT)
N_EPI, N_PREP, N_THOUGHT = 8, 3, len(THOUGHT)
PROJECT = {(0, "A"): "K", (0, "B"): "E", (1, "A"): 0, (1, "B"): 1, (2, "A"): 2, (3, "A"): 3}
PROJECT_LAST = {(1, "A"): "K", (1, "B"): "E", (2, "A"): 0, (2, "B"): 1, (3, "A"): 2, (3, "B"): 3}
PJOBS = ["K", "E", 0, 1, 2, 3]
THOUGHT_AT = [(6, "A"), (6, "B")] + [(7 + 2 * n + m // 2, "AB"[m % 2]) for n in range(STEPS) for m in range(3)]
THOUGHT_AT += [(14, "C"), (15, "A"), (15, "B"), (15, "C")]
FINAL_AFTER = [0, 1, 2, 4, 5]


def plan(it, kind):
    steps = {(1, "A"): [("V", it)]}

    def add(at, names, arg):
        steps.setdefault(at, []).extend((n, arg) for n in names)

    if kind != "first":
        for at, names in EPILOGUE.items():
            add(at, names, it - 1)
    if kind == "thought":
        for n, name in enumerate(THOUGHT):
            add(THOUGHT_AT[n], [name], n)
    if kind in ("final", "last"):
        for n, name in enumerate(FINAL):
            add((FINAL_AFTER[n], "C"), [name], ("S", it - 5, (it - 5) * 2))
            add((6 + FINAL_AFTER[n], "C"), [name], ("E", it - 1, (it - 5) * 2 + 1))
    if kind == "last":
        for n, name in enumerate(FINAL[:3]):
            add((12 + n, "C"), [name], ("S", 3, 6))
    if kind != "last":
        for at, names in PREPARE.items():
            add(at, names, it + 1)
    return steps


def misc_base(it):
    if isinstance(it, int) and it == 0:
        return N_PREP
    return it * (1 + N_EPI + N_PREP) - N_EPI + N_PREP


def build(nc, x_steps, w_all, wo_t, gate_t, agg_t, bc_t, d1_t, d2_t, d1b_t, vec128, vec4, rope, mask_std,
          mask_edge, ident_bf, ident_f, select, out):
    f32, f32r, bf16 = mybir.dt.float32, mybir.dt.float32r, mybir.dt.bfloat16
    ACT = mybir.ActivationFunctionType
    AX = mybir.AxisListType
    ctx = ExitStack()
    with ctx:
        sb = lambda n, s, d=f32: ctx.enter_context(nc.sbuf_tensor(n, s, d))
        ps = lambda n, s: ctx.enter_context(nc.psum_tensor(n, s, f32))
        sem = lambda n: ctx.enter_context(nc.semaphore(n))

        w_hi, w_lo = sb("w_hi", [P, KT, WALL], f32r), sb("w_lo", [P, KT, WALL], f32r)
        wo_sb, gate_w = sb("wo_sb", [P, KT, D]), sb("gate_w", [P, KT, D])
        agg_w, bc_w = sb("agg_w", [P, KT, D]), sb("bc_w", [P, KT, D])
        d1_w, d2_w, d1_b = sb("d1_w", [P, KT, H]), sb("d2_w", [P, HT, D]), sb("d1_b", [P, HT])
        v128, v4 = sb("v128", [P, 3, D]), sb("v4", [BATCH, 7, D])
        gate_b, out_gamma, out_beta = (v128[:, n, :] for n in range(3))
        in_gamma, in_beta, agg_b, pn_gamma, pn_beta, d2_b, bc_b = (v4[:, n, :] for n in range(7))
        rope_sb = sb("rope_sb", [P, 2, XW])
        std_sb, edge_sb = sb("std_sb", [P, 2 * BLK], bf16), sb("edge_sb", [P, 2, KEYS], bf16)
        id_bf, id_f, sel = sb("id_bf", [P, P], bf16), sb("id_f", [P, P]), sb("sel", [BATCH, BATCH, P])
        x_in = sb("x_in", [P, 1 + TILES, D])
        x_hi, x_lo = sb("x_hi", [P, KT, XW], f32r), sb("x_lo", [P, KT, XW], f32r)
        rope_c, rope_s = sb("rope_c", [P, 2, CHUNK]), sb("rope_s", [P, 2, CHUNK])
        q_sb = sb("q_sb", [P, 2, 2, NBLK, P])
        k_ext, k_sb = sb("k_ext", [P, EXT]), sb("k_sb", [P, 2, NBLK, KEYS])
        v_sb, vf_sb = sb("v_sb", [P, NBLK, GROUPS, VW]), sb("vf_sb", [P, GROUPS, 4 * VW])
        neg_max = sb("neg_max", [P, 4, 2])
        prob = sb("prob", [P, 2, 4, KEYS])
        prob_f = sb("prob_f", [P, 2, 4, FRONT])
        prob_t = sb("prob_t", [P, 2, 5 * P])
        rcp, o_sb = sb("rcp", [P, 2, 4]), sb("o_sb", [P, NBLK, P])
        e_t = sb("e_t", [P, KT, CHUNK])
        y, x1, z = sb("y", [P, TILES, D]), sb("x1", [P, TILES, D]), sb("z", [P, TILES, D])
        store = sb("store", [P, 2, NSTORE, TILES * D])
        stats, mv = sb("stats", [P, TILES, 6]), sb("mv", [P, TILES, 2])
        rstd, half_pow = sb("rstd", [P, 2, TILES]), sb("half_pow", [P, TILES])
        eps1, eps2 = sb("eps1", [P, TILES]), sb("eps2", [P, TILES])
        carry = sb("carry", [1, 1])
        f1 = d1_w[:, 0, :].rearrange("p (t d) -> p t d", t=TILES)
        f2 = d1_w[:, 1, :].rearrange("p (t d) -> p t d", t=TILES)
        fstats, fmv, frstd = sb("fstats", [P, TILES, 6]), sb("fmv", [P, TILES, 2]), sb("frstd", [P, 2, TILES])
        bc_sb = sb("bc_sb", [P, BATCH, D])
        last_x, th = sb("last_x", [BATCH, D]), sb("th", [BATCH, D])
        tn, tst, tmv, trs = sb("tn", [BATCH, D]), sb("tst", [BATCH, 6]), sb("tmv", [BATCH, 2]), sb("trs", [BATCH, 2])
        t_t, hid, hid_g = sb("t_t", [P, KT, BATCH]), sb("hid", [P, HT, BATCH]), sb("hid_g", [P, HT, BATCH])
        stage_w = store[:, :, :, :].rearrange("p a n d -> p (a n d)")[:, 0:KT * WALL].rearrange("p (k n) -> p k n", k=KT)

        pj = [ps(f"pj{n}", [P, 512]) for n in range(2)]
        s_ps = [ps(f"s_ps{n}", [P, 512]) for n in range(2)]
        pt_ps, pf_ps = ps("pt_ps", [P, 512]), ps("pf_ps", [P, 512])
        pv_ps, misc = ps("pv_ps", [P, 512]), ps("misc", [P, 512])
        v_ps = [misc[:, t * GROUPS * DV:(t + 1) * GROUPS * DV] for t in range(TILES + 1)]

        w_loaded, c_loaded, ffn_loaded = [sem(f"w_loaded{k}") for k in range(KT)], sem("c_loaded"), sem("ffn_loaded")
        x_loaded, rope_loaded, edge_loaded, res_loaded = sem("x_loaded"), sem("rope_loaded"), sem("edge_loaded"), sem("res_loaded")
        const_step, const_set, hi_split, w_split = sem("const_step"), sem("const_set"), sem("hi_split"), sem("w_split")
        proj_done, rope_mul, rope_add, k_ready = sem("proj_done"), sem("rope_mul"), sem("rope_add"), sem("k_ready")
        s_done, max_done, exp_done = sem("s_done"), sem("max_done"), sem("exp_done")
        t_done, pt_ready, pv_done, rcp_done, o_ready, front_ready = sem("t_done"), sem("pt_ready"), sem("pv_done"), sem("rcp_done"), sem("o_ready"), sem("front_ready")
        misc_done, misc_read, xhi_ready = sem("misc_done"), sem("misc_read"), sem("xhi_ready")
        bn_done, mv_ready, ve_ready, rstd_ready, x1_ready = sem("bn_done"), sem("mv_ready"), sem("ve_ready"), sem("rstd_ready"), sem("x1_ready")
        tanh_ready, x1_stored, tail_x = sem("tanh_ready"), sem("x1_stored"), sem("tail_x")
        f_gated, f_sum, f_bn, f_mv, f_ve, f_rstd = sem("f_gated"), sem("f_sum"), sem("f_bn"), sem("f_mv"), sem("f_ve"), sem("f_rstd")
        f_norm, f_scaled, f_added, stored = sem("f_norm"), sem("f_scaled"), sem("f_added"), sem("stored")
        th_rows, th_mv, th_ve, th_rstd = sem("th_rows"), sem("th_mv"), sem("th_ve"), sem("th_rstd")
        th_link, gelu_ready = sem("th_link"), sem("gelu_ready")

        S_N, Q_N, P_N = 32, 16, 24
        P_FIRST = len(PJOBS)

        def thought_jobs(kind):
            return N_THOUGHT if kind in ("final", "last", "tail") else 0

        def walk(kind, it, place, state):
            for name, arg in state["steps"].get(place, []):
                idx = state["base"] + state["n"]
                if name in MISC_JOBS:
                    state["n"] += 1
                yield name, arg, idx

        def state_of(it, kind):
            return {"steps": plan(it, kind), "base": misc_base(it) + thought_jobs(kind), "n": 0}

        def columns(what):
            return {"K": (0, KSPLIT), "E": (KSPLIT, XW)}.get(what, (EXT, XW))

        def proj_at(g, j, place):
            table = PROJECT_LAST if g == 3 else PROJECT
            what = table.get((j, place))
            return None if what is None else (6 * g + PJOBS.index(what), what)

        def chunks(eng, body):
            body(0, "first")
            with eng.Fori(1, 4) as it:
                body(it, "store")
            body(4, "thought")
            with eng.Fori(5, 7) as it:
                body(it, "final")
            body(7, "last")

        tail_plan = [(n, ("S", 3, 6)) for n in FINAL[3:]] + [(n, 7) for n in ("OT0", "OT1", "OP0", "OP1", "BN", "NM", "X1T0", "X1T1", "G0", "G1")]
        tail_plan += [(n, ("E", 7, 7)) for n in FINAL]

        def tail_steps():
            idx = misc_base(7) + N_THOUGHT + 1 + N_EPI
            for name, arg in tail_plan:
                yield name, arg, idx
                if name in MISC_JOBS:
                    idx += 1

        thought_over = misc_base(5) + N_THOUGHT

        def sources(src, n):
            if src == "S":
                at = bass.ds(n, 1)
                xs, ts = (store[:, k, at, :].rearrange("p a (t d) -> p (a t) d", t=TILES) for k in range(2))
                return xs, ts, bc_sb[:, at, :]
            return x1[:, :, :], z[:, :, :], bc_sb[:, bass.ds(n - NSTORE, 1), :]

        block = ctx.enter_context(nc.Block())

        @block.sync
        def _(sp):
            def load_x(n):
                sp.dma_start(x_in[0:EXT, 0, :], x_steps[bass.ds(n, 1), 0:EXT, :].rearrange("a p d -> (a p) d")).then_inc(x_loaded, 16)
                sp.dma_start(x_in[:, 1:, :], x_steps[bass.ds(n, 1), EXT:XW, :].rearrange("a (t p) d -> (a p) t d", p=P)).then_inc(x_loaded, 16)

            def load_rope(n, half):
                sp.dma_start(rope_sb[:], rope[bass.ds(half, 1)].rearrange("a p c n -> (a p) c n")).then_inc(rope_loaded, 16)

            def load_edge(half):
                sp.dma_start(edge_sb[:], mask_edge[bass.ds(half, 1)].rearrange("a p u n -> (a p) u n")).then_inc(edge_loaded, 16)

            sp.dma_start(id_f[:], ident_f).then_inc(c_loaded, 16)
            load_x(0)
            sp.dma_start(stage_w[:, 0, :], w_all[:, 0, :]).then_inc(w_loaded[0], 16)
            sp.dma_start(stage_w[:, 1, :], w_all[:, 1, :]).then_inc(w_loaded[1], 16)
            load_rope(0, 0)
            sp.dma_start(id_bf[:], ident_bf).then_inc(c_loaded, 16)
            sp.dma_start(std_sb[:], mask_std).then_inc(c_loaded, 16)
            load_edge(0)
            for dst, src in ((wo_sb, wo_t), (gate_w, gate_t), (agg_w, agg_t), (bc_w, bc_t), (d1_w, d1_t),
                             (d2_w, d2_t), (d1_b, d1b_t), (v128, vec128), (v4, vec4), (sel, select)):
                sp.dma_start(dst[:], src).then_inc(ffn_loaded, 16)

            def body(it, kind):
                base = misc_base(it) + thought_jobs(kind)
                if kind != "last":
                    sp.wait_ge(misc_done, base)
                    load_x(it + 1)
                    sp.wait_ge(rope_mul, it * P_N + P_N)
                    half = {"first": 0, "thought": 1, "final": 1}.get(kind)
                    nxt = half if half is not None else (it + 1) // NSTORE
                    load_rope(it + 1, nxt)
                if kind != "first":
                    sp.wait_ge(x1_ready, it)
                sp.dma_start(y[:], x_steps[bass.ds(it, 1), EXT:XW, :].rearrange("a (t p) d -> (a p) t d", p=P)).then_inc(res_loaded, 16)
                if kind != "last":
                    sp.wait_ge(s_done, it * S_N + 3 * 8 + 2)
                    load_edge(nxt)

            chunks(sp, body)

        @block.tensor
        def _(pe):
            mm = nc.tensor.matmul

            def split_mm(o, w, x):
                for k in range(KT):
                    for n, (a, b) in enumerate(((w_hi, x_hi), (w_hi, x_lo), (w_lo, x_hi))):
                        last = mm(o, w(a, k), x(b, k), start=(k == 0 and n == 0), stop=(k == KT - 1 and n == 2))
                return last

            def project(idx, g, what):
                if not (isinstance(idx, int) and idx < 2):
                    pe.wait_ge(rope_mul, idx - 1)
                bank = pj[PJOBS.index(what) % 2]
                col = (WK0 + g * P) if what in ("K", "E") else WQ0 + (g * REP + what) * P
                lo, hi = columns(what)
                split_mm(bank[:, 0:hi - lo], lambda a, k: a[:, k, col:col + P],
                         lambda b, k: b[:, k, lo:hi]).then_inc(proj_done, 1)

            def scores(it, g, j, pair):
                pe.wait_ge(rope_add, it * P_N + g * P_FIRST + 2 * pair + 4)
                if pair == 0:
                    pe.wait_ge(k_ready, it * GROUPS + g + 1)
                if not (isinstance(it, int) and it == 0 and g == 0 and j == 0):
                    pe.wait_ge(exp_done, it * S_N + g * 8 + 2 * j + pair - 1)
                if j == 0 and pair == 0 and g == 0:
                    pe.wait_ge(edge_loaded, it * 16 + 16)
                bank = s_ps[pair][:, 0:2 * KEYS].rearrange("p (u n) -> p u n", u=2)
                for u in range(2):
                    blk = 2 * j + u
                    mm(bank[:, u, :], q_sb[:, g % 2, pair, blk, :],
                       k_sb[:, g % 2, blk, :], start=(u == 0), stop=False)
                if j == 0:
                    last = mm(bank, id_bf[:], edge_sb[:], start=False, stop=True)
                else:
                    last = mm(bank[:, :, FRONT:], id_bf[:], std_sb[:, None, :].broadcast_to([P, 2, 2 * BLK]), start=False, stop=True)
                last.then_inc(s_done, 1)

            def transposes(quad, par):
                pe.wait_ge(front_ready, quad + 1)
                if not (isinstance(quad, int) and quad == 0):
                    pe.wait_ge(pt_ready, quad)
                for n in range(4):
                    nc.tensor.transpose(pt_ps[:, n * P:(n + 1) * P], prob[:, par, n, FRONT:], id_f[:])
                nc.tensor.transpose(pf_ps[:, 0:P], prob_f[:, par, :, :].rearrange("p n k -> p (n k)"), id_f[:]).then_inc(t_done, 1)

            def values(quad, par, g, j):
                pe.wait_ge(pt_ready, quad + 1)
                if not (isinstance(quad, int) and quad == 0):
                    pe.wait_ge(o_ready, quad)
                mm(pv_ps[:, 0:4 * VW], prob_t[:, par, 4 * P:], vf_sb[:, g, :], start=True, stop=False)
                for n in range(4):
                    last = mm(pv_ps[:, n * VW:(n + 1) * VW], prob_t[:, par, n * P:(n + 1) * P],
                              v_sb[:, 2 * j + n % 2, g, :], start=False, stop=(n == 3))
                last.then_inc(pv_done, 1)

            def to_misc(idx):
                if not (isinstance(idx, int) and idx == 0):
                    pe.wait_ge(misc_read, idx)

            def step(name, arg, idx):
                if name not in MISC_JOBS:
                    return
                to_misc(idx)
                if name == "V":
                    for t in range(TILES + 1):
                        at = EXT + t * P if t < TILES else 0
                        last = split_mm(v_ps[t], lambda a, k: x_hi[:, k, at:at + P] if a is w_hi else x_lo[:, k, at:at + P],
                                        lambda b, k: w_hi[:, k, WV0:WALL] if b is x_hi else w_lo[:, k, WV0:WALL])
                elif name in ("XT0", "XT1", "XTE"):
                    if name == "XT0":
                        pe.wait_ge(x_loaded, arg * 32 + 32)
                    if name == "XTE":
                        for k in range(KT):
                            last = nc.tensor.transpose(misc[:, k * EXT:(k + 1) * EXT], x_in[0:EXT, 0, k * P:(k + 1) * P], id_f[0:EXT, 0:EXT])
                    else:
                        k = int(name[2])
                        for t in range(TILES):
                            last = nc.tensor.transpose(misc[:, t * P:(t + 1) * P], x_in[:, 1 + t, k * P:(k + 1) * P], id_f[:])
                elif name in ("OT0", "OT1"):
                    pe.wait_ge(o_ready, arg * Q_N + Q_N)
                    for u in range(4):
                        last = nc.tensor.transpose(misc[:, u * P:(u + 1) * P], o_sb[:, 4 * int(name[2]) + u, :], id_f[:])
                elif name in ("OP0", "OP1", "G0", "G1"):
                    a, w = int(name[-1]), wo_sb if name[0] == "O" else gate_w
                    for t in range(2):
                        for k in range(KT):
                            last = mm(misc[:, t * D:(t + 1) * D], e_t[:, k, (2 * a + t) * P:(2 * a + t + 1) * P], w[:, k, :],
                                      start=(k == 0), stop=(k == KT - 1))
                elif name in ("X1T0", "X1T1"):
                    pe.wait_ge(x1_ready, arg + 1)
                    k = int(name[3])
                    for t in range(TILES):
                        last = nc.tensor.transpose(misc[:, t * P:(t + 1) * P], x1[:, t, k * P:(k + 1) * P], id_f[:])
                elif name in ("TN", "TT", "TU"):
                    pe.wait_ge(th_rows, {"TN": 1, "TU": 2 + STEPS}.get(name, 2 + (arg - 2) // 3))
                    rows = th if name == "TU" else tn
                    for k in range(KT):
                        last = nc.tensor.transpose(misc[:, k * BATCH:(k + 1) * BATCH], rows[:, k * P:(k + 1) * P], id_f[0:BATCH, 0:BATCH])
                elif name in ("TA", "TB"):
                    for k in range(KT):
                        last = mm(misc[0:BATCH, 0:D], t_t[:, k, :], (agg_w if name == "TA" else bc_w)[:, k, :], start=(k == 0), stop=(k == KT - 1))
                elif name == "TH":
                    for m in range(HT):
                        for k in range(KT):
                            last = mm(misc[:, m * BATCH:(m + 1) * BATCH], d1_w[:, k, m * P:(m + 1) * P], t_t[:, k, :], start=(k == 0), stop=(k == KT - 1))
                elif name == "TD":
                    pe.wait_ge(gelu_ready, (arg - 2) // 3 + 1)
                    for m in range(HT):
                        last = mm(misc[0:BATCH, 0:D], hid_g[:, m, :], d2_w[:, m, :], start=(m == 0), stop=(m == HT - 1))
                else:
                    for b in range(2):
                        last = mm(misc[:, b * D:(b + 1) * D], sel[:, 2 * int(name[2]) + b, :], tn[:, :], start=True, stop=True)
                last.then_inc(misc_done, 1)

            pe.wait_ge(c_loaded, 48)
            for n, name in enumerate(("XT0", "XT1", "XTE")):
                step(name, 0, n)
            pe.wait_ge(misc_read, N_PREP)
            pe.wait_ge(w_split, 2)
            for n, what in enumerate(PJOBS):
                project(n, 0, what)
            pe.wait_ge(ffn_loaded, 160)
            pe.wait_ge(const_set, 1)

            def body(it, kind):
                st = state_of(it, kind)
                x_read = None
                for q in range(Q_N):
                    g, j = q // 4, q % 4
                    quad = it * Q_N + q
                    for pair, place in ((0, "A"), (1, "B")):
                        scores(it, g, j, pair)
                        if pair == 0 and (kind != "first" or q >= 2):
                            if q == 2:
                                pe.wait_ge(misc_read, st["base"] + 1)
                            values(quad - 2, q % 2, (q - 2) % Q_N // 4, (q - 2) % 4)
                        for name, arg, idx in walk(kind, it, (q, place), st):
                            step(name, arg, idx)
                            if name == "XTE":
                                x_read = idx + 1
                        p = proj_at(g, j, place)
                        if p and not (kind == "last" and g == 3):
                            if p[0] == 18:
                                pe.wait_ge(misc_read, x_read)
                            project(P_FIRST + it * P_N + p[0], (g + 1) % 4, p[1])
                        if pair == 0 and (kind != "first" or q >= 1):
                            transposes(quad - 1, (q - 1) % 2)
                    for name, arg, idx in walk(kind, it, (q, "C"), st):
                        step(name, arg, idx)
                        if name == "XTE":
                            x_read = idx + 1

            chunks(pe, body)
            values(NCH * Q_N - 2, 0, 3, 2)
            transposes(NCH * Q_N - 1, 1)
            values(NCH * Q_N - 1, 1, 3, 3)
            for name, arg, idx in tail_steps():
                step(name, arg, idx)

        @block.vector
        def _(dve):
            v = nc.vector

            def rotate(idx, what):
                dve.wait_ge(proj_done, idx + 1)
                if not (isinstance(idx, int) and idx < 2):
                    dve.wait_ge(rope_add, idx - 1)
                par = PJOBS.index(what) % 2
                lo, hi = columns(what)
                n, half = hi - lo, P // 2
                v.tensor_tensor(rope_c[:, par, 0:n], pj[par][:, 0:n], rope_sb[:, 0, lo:hi], ALU.mult)
                v.tensor_tensor(rope_s[half:P, par, 0:n], pj[par][0:half, 0:n], rope_sb[0:half, 1, lo:hi], ALU.mult)
                v.tensor_tensor(rope_s[0:half, par, 0:n], pj[par][half:P, 0:n], rope_sb[half:P, 1, lo:hi], ALU.mult).then_inc(rope_mul, 1)

            def row_max(idx, pair, slot):
                dve.wait_ge(s_done, idx + 1)
                v.tensor_reduce(out=neg_max[:, slot, :], in_=s_ps[pair][:, 0:2 * KEYS].rearrange("p (u n) -> p u n", u=2),
                                axis=AX.X, op=ALU.max, negate=True).then_inc(max_done, 1)

            def normalize(quad, par):
                dve.wait_ge(pv_done, quad + 1)
                units = pv_ps[:, 0:4 * VW].rearrange("p (n e) -> p n e", e=VW)
                v.reciprocal(rcp[:, par, :], units[:, :, DV]).then_inc(rcp_done, 1)

            def normalize_out(quad, par, g, j):
                dve.wait_ge(rcp_done, quad + 1)
                units = pv_ps[:, 0:4 * VW].rearrange("p (r u e) -> p r u e", r=2, e=VW)
                dst = o_sb[:, 2 * j:2 * j + 2, g * 2 * DV:(g + 1) * 2 * DV].rearrange("p u (r d) -> p r u d", r=2)
                v.tensor_tensor(dst, units[:, :, :, 0:DV], rcp[:, par, :].rearrange("p (r u) -> p r u", r=2)[:, :, :, None].broadcast_to([P, 2, 2, DV]),
                                ALU.mult).then_inc(o_ready, 1)

            def layer_norm4(dst, src, st, m, bn, mvs):
                for t in range(TILES):
                    last = v.bn_stats(st[:, t, :], src[:, t, :])
                last.then_inc(bn[0], 1)
                dve.wait_ge(bn[0], bn[1])
                v.memset(carry[:], 0.0)
                for t in range(TILES):
                    last = v.bn_aggr(m[:, t, :], st[:, t, :])
                last.then_inc(mvs, 1)

            def th_norm(rows, gamma, beta, n):
                v.bn_stats(tst[:], rows).then_inc(th_link, 1)
                chain()
                v.bn_aggr(tmv[:], tst[:]).then_inc(th_mv, 1)
                dve.wait_ge(th_rstd, n + 1)
                v.tensor_scalar(out=tn[:], in0=rows, scalar1=tmv[:, 0:1], scalar2=trs[:, 1:2], op0=ALU.subtract, op1=ALU.mult).then_inc(th_link, 1)
                chain()
                v.tensor_tensor(tn[:], tn[:], gamma, ALU.mult).then_inc(th_link, 1)
                chain()
                v.tensor_tensor(tn[:], tn[:], beta, ALU.add).then_inc(th_rows, 1)

            links = [0]

            def chain():
                links[0] += 1
                dve.wait_ge(th_link, links[0])

            def step(name, arg, idx):
                if name in MISC_JOBS and name not in ("OT0", "OT1", "X1T0", "X1T1"):
                    dve.wait_ge(misc_done, idx + 1)
                if name == "V":
                    if not (isinstance(arg, int) and arg == 0):
                        dve.wait_ge(pv_done, arg * Q_N)
                    else:
                        dve.wait_ge(const_set, 1)
                    half, own = P // 2, misc[:, 0:TILES * GROUPS * DV].rearrange("p (t g d) -> p t g d", t=TILES, g=GROUPS)
                    ext = v_ps[TILES].rearrange("p (g d) -> p g d", g=GROUPS)
                    v.tensor_copy(v_sb[:, 1::2, :, 0:DV], own)
                    v.tensor_copy(v_sb[half:P, 0::2, :, 0:DV], own[0:half])
                    v.tensor_copy(v_sb[0:half, 2::2, :, 0:DV], own[half:P, 0:TILES - 1])
                    v.tensor_copy(v_sb[0:half, 0, :, 0:DV], ext[0:half])
                    for n in range(4):
                        last = v.tensor_copy(vf_sb[n * FRONT:(n + 1) * FRONT, :, n * VW:n * VW + DV], ext[BLK:EXT])
                    last.then_inc(misc_read, 1)
                elif name in ("XT0", "XT1", "XTE"):
                    dve.wait_ge(xhi_ready, arg * 3 + ("XT0", "XT1", "XTE").index(name) + 1)
                    if name == "XTE":
                        dst, hi, src = x_lo[:, :, 0:EXT], x_hi[:, :, 0:EXT], misc[:, 0:KT * EXT].rearrange("p (k n) -> p k n", k=KT)
                    else:
                        k = int(name[2])
                        dst, hi, src = x_lo[:, k, EXT:], x_hi[:, k, EXT:], misc[:, :]
                    v.tensor_tensor(dst, src, hi.bitcast(f32), ALU.subtract).then_inc(misc_read, 1)
                elif name in ("OP0", "OP1"):
                    a = int(name[2])
                    if a == 0:
                        dve.wait_ge(res_loaded, arg * 16 + 16)
                    v.tensor_tensor(y[:, 2 * a:2 * a + 2, :], misc[:, :].rearrange("p (t d) -> p t d", t=2), y[:, 2 * a:2 * a + 2, :], ALU.add).then_inc(misc_read, 1)
                    if a == 1:
                        last_res[0] = idx + 1
                elif name == "BN":
                    dve.wait_ge(misc_read, last_res[0])
                    layer_norm4(None, y, stats, mv, (bn_done, arg + 1), mv_ready)
                elif name == "NM":
                    dve.wait_ge(rstd_ready, arg + 1)
                    if not (isinstance(arg, int) and arg == 0):
                        free_x1(arg)
                    for t in range(TILES):
                        last = v.tensor_scalar(out=x1[:, t, :], in0=y[:, t, :], scalar1=mv[:, t, 0:1], scalar2=rstd[:, 1, t:t + 1],
                                               op0=ALU.subtract, op1=ALU.mult)
                    last.then_inc(x1_ready, 1)
                elif name in ("G0", "G1"):
                    a = int(name[1])
                    if a == 0:
                        free_z(arg)
                    v.tensor_tensor(z[:, 2 * a:2 * a + 2, :], misc[:, :].rearrange("p (t d) -> p t d", t=2),
                                    gate_b[:, None, :].broadcast_to([P, 2, D]), ALU.add).then_inc(misc_read, 1)
                elif name in FINAL:
                    final(name, *arg)
                elif name in THOUGHT:
                    thought(name, arg, idx)

            last_res = [0]
            state = {"kind": None}

            def free_x1(arg):
                if state["kind"] in ("store", "thought"):
                    dve.wait_ge(x1_stored, arg * 16)
                else:
                    dve.wait_ge(x1_stored, NSTORE * 16)
                    dve.wait_ge(f_added, (arg - NSTORE) * 2 + 1)

            def free_z(arg):
                if isinstance(arg, int) and arg == 0:
                    return
                dve.wait_ge(tanh_ready, arg * 2)
                if state["kind"] not in ("store", "thought"):
                    dve.wait_ge(f_gated, (arg - NSTORE) * 2 + 1)

            def final(name, src, n, fi):
                xs, ts, b = sources(src, n)
                if name == "FA":
                    if src == "E":
                        dve.wait_ge(tanh_ready, n * 2 + 2)
                    else:
                        dve.wait_ge(tanh_ready, n * 2 + 2)
                    dve.wait_ge(misc_read, thought_over)
                    dve.wait_ge(stored, fi * 16 + 16)
                    v.scalar_tensor_tensor(out=f1, in0=ts, scalar=1.0, in1=b.broadcast_to([P, TILES, D]), op0=ALU.add, op1=ALU.mult).then_inc(f_gated, 1)
                elif name in ("FB", "FD"):
                    first = name == "FB"
                    dve.wait_ge(f_sum if first else f_added, fi + (1 if first else 2))
                    layer_norm4(None, f1 if first else f2, fstats, fmv, (f_bn, 2 * fi + (1 if first else 2)), f_mv)
                else:
                    first = name == "FC"
                    dve.wait_ge(f_rstd, 2 * fi + (1 if first else 2))
                    a, o = (f1, f2) if first else (f2, f1)
                    for t in range(TILES):
                        last = v.tensor_scalar(out=o[:, t, :], in0=a[:, t, :], scalar1=fmv[:, t, 0:1], scalar2=frstd[:, 1, t:t + 1], op0=ALU.subtract, op1=ALU.mult)
                    last.then_inc(f_norm, 1)

            def thought(name, n, idx):
                rows = misc[0:BATCH, 0:D]
                if name in ("TN", "TT", "TU"):
                    v.tensor_copy(t_t[:, :, :], misc[:, 0:KT * BATCH].rearrange("p (k b) -> p k b", k=KT)).then_inc(misc_read, 1)
                elif name == "TA":
                    v.tensor_tensor(th[:], rows, agg_b, ALU.add).then_inc(misc_read, 1)
                    dve.wait_ge(misc_read, idx + 1)
                    th_norm(th[:], pn_gamma, pn_beta, 1)
                elif name == "TH":
                    v.tensor_tensor(hid[:], misc[:, 0:HT * BATCH].rearrange("p (m b) -> p m b", m=HT), d1_b[:, :, None].broadcast_to([P, HT, BATCH]), ALU.add).then_inc(misc_read, 1)
                elif name == "TD":
                    s = (n - 2) // 3
                    v.tensor_tensor(tn[:], rows, d2_b, ALU.add).then_inc(misc_read, 1)
                    dve.wait_ge(misc_read, idx + 1)
                    last = v.tensor_tensor(th[:], th[:], tn[:], ALU.add)
                    if s < STEPS - 1:
                        last.then_inc(th_link, 1)
                        chain()
                        th_norm(th[:], pn_gamma, pn_beta, 2 + s)
                    else:
                        last.then_inc(th_rows, 1)
                elif name == "TB":
                    v.tensor_tensor(tn[:], rows, bc_b, ALU.add).then_inc(misc_read, 1)
                else:
                    a = int(name[2])
                    v.tensor_copy(bc_sb[:, 2 * a:2 * a + 2, :], misc[:, :].rearrange("p (b d) -> p b d", b=2)).then_inc(misc_read, 1)

            v.memset(vf_sb[:], 0.0).then_inc(const_step, 1)
            dve.wait_ge(const_step, 1)
            for n in range(4):
                v.memset(vf_sb[n * FRONT:(n + 1) * FRONT, :, n * VW + DV:(n + 1) * VW], 1.0)
            v.memset(eps1[:], EPS1)
            v.memset(eps2[:], EPS2)
            v.memset(frstd[:], 0.0).then_inc(f_gated, 1)
            v.memset(half_pow[:], -0.5).then_inc(f_added, 1)
            v.memset(carry[:], 0.0).then_inc(stored, 16)
            v.memset(v_sb[:, :, :, DV:VW], 1.0).then_inc(const_set, 1)
            for k in range(KT):
                dve.wait_ge(hi_split, k + 1)
                v.tensor_tensor(w_lo[:, k, :], stage_w[:, k, :], w_hi[:, k, :].bitcast(f32), ALU.subtract).then_inc(w_split, 1)
            for n, name in enumerate(("XT0", "XT1", "XTE")):
                step(name, 0, n)
            dve.wait_ge(rope_loaded, 16)
            for n, what in enumerate(PJOBS):
                rotate(n, what)

            def body(it, kind):
                state["kind"] = kind
                st = state_of(it, kind)
                for q in range(Q_N):
                    g, j = q // 4, q % 4
                    quad = it * Q_N + q
                    for pair, place in ((0, "A"), (1, "B")):
                        row_max(it * S_N + q * 2 + pair, pair, (q * 2 + pair) % 4)
                        if pair == 0 and (kind != "first" or q >= 2):
                            normalize(quad - 2, q % 2)
                            if q == 2 and kind != "first":
                                dve.wait_ge(misc_done, st["base"] + 3)
                            normalize_out(quad - 2, q % 2, (q - 2) % Q_N // 4, (q - 2) % 4)
                        for name, arg, idx in walk(kind, it, (q, place), st):
                            step(name, arg, idx)
                        p = proj_at(g, j, place)
                        if p and not (kind == "last" and g == 3):
                            if p[0] == 18:
                                dve.wait_ge(rope_loaded, it * 16 + 32)
                            rotate(P_FIRST + it * P_N + p[0], p[1])
                    for name, arg, idx in walk(kind, it, (q, "C"), st):
                        step(name, arg, idx)
                    if kind == "thought" and q == THOUGHT_AT[0][0] - 1:
                        dve.wait_ge(tail_x, 16)
                        th_norm(last_x[:], in_gamma, in_beta, 0)

            chunks(dve, body)
            state["kind"] = "tail"
            for n in (2, 1):
                normalize(NCH * Q_N - n, n % 2)
                normalize_out(NCH * Q_N - n, n % 2, 3, 4 - n)
            for name, arg, idx in tail_steps():
                step(name, arg, idx)

        @block.scalar
        def _(act):
            sc = nc.scalar

            def exps(quad, q, pair):
                idx = 2 * quad + pair
                act.wait_ge(max_done, idx + 1)
                if not (isinstance(quad, int) and quad < 2):
                    act.wait_ge(t_done, quad - 1)
                for u in range(2):
                    last = sc.activation(prob[:, q % 2, 2 * pair + u, :], s_ps[pair][:, u * KEYS:(u + 1) * KEYS], ACT.Exp,
                                         bias=neg_max[:, (q * 2 + pair) % 4, u:u + 1], scale=1.0)
                last.then_inc(exp_done, 1)

            def gather_front(quad, q):
                act.wait_ge(exp_done, 2 * quad + 2)
                sc.copy(prob_f[:, q % 2, :, :], prob[:, q % 2, :, 0:FRONT]).then_inc(front_ready, 1)

            def copy_transposed(quad, par):
                act.wait_ge(t_done, quad + 1)
                if not (isinstance(quad, int) and quad < 2):
                    act.wait_ge(pv_done, quad - 1)
                sc.copy(prob_t[:, par, 0:4 * P], pt_ps[:, :])
                sc.copy(prob_t[:, par, 4 * P:], pf_ps[:, 0:P]).then_inc(pt_ready, 1)

            def spread_keys(stage, par):
                act.wait_ge(rope_add, stage * P_FIRST + 2)
                sc.copy(k_sb[:, par, 0, FRONT:FRONT + BLK], k_ext[:, 0:BLK])
                sc.copy(k_sb[:, par, 1:, FRONT:FRONT + BLK], k_sb[:, par, 0:NBLK - 1, FRONT + BLK:])
                sc.copy(k_sb[:, par, :, 0:FRONT], k_ext[:, None, BLK:].broadcast_to([P, NBLK, FRONT])).then_inc(k_ready, 1)

            def step(name, arg, idx, kind):
                if name in ("OT0", "OT1", "X1T0", "X1T1", "XT0", "XT1", "XTE"):
                    act.wait_ge(misc_done, idx + 1)
                if name in ("XT0", "XT1", "XTE"):
                    if name == "XT0" and not (isinstance(arg, int) and arg == 0):
                        act.wait_ge(proj_done, arg * P_N)
                    if name == "XTE":
                        sc.copy(x_hi[:, :, 0:EXT], misc[:, 0:KT * EXT].rearrange("p (k n) -> p k n", k=KT)).then_inc(xhi_ready, 1)
                    else:
                        sc.copy(x_hi[:, int(name[2]), EXT:], misc[:, :]).then_inc(xhi_ready, 1)
                elif name in ("OT0", "OT1"):
                    a = int(name[2])
                    dst = e_t[:, :, a * 4 * BLK:(a + 1) * 4 * BLK].rearrange("p h (u q) -> p h u q", u=4)
                    sc.copy(dst, misc[:, :].rearrange("p (u h q) -> p h u q", u=4, h=2)).then_inc(misc_read, 1)
                elif name in ("X1T0", "X1T1"):
                    sc.copy(e_t[:, int(name[3]), :], misc[:, :]).then_inc(misc_read, 1)
                elif name == "NM" and kind in ("store", "thought"):
                    act.wait_ge(x1_ready, arg + 1)
                    act.dma_start(store[:, 0, bass.ds(arg, 1), :].rearrange("p a d -> p (a d)"),
                                  x1[:, :, :].rearrange("p t d -> p (t d)")).then_inc(x1_stored, 16)
                elif name in ("G0", "G1"):
                    act.wait_ge(misc_read, idx + 1)
                    a = int(name[1])
                    src = z[:, 2 * a:2 * a + 2, :].rearrange("p t d -> p (t d)")
                    dst = src
                    if kind in ("store", "thought"):
                        dst = store[:, 1, bass.ds(arg, 1), a * 2 * D:(a + 1) * 2 * D].rearrange("p a d -> p (a d)")
                    sc.activation(dst, src, ACT.Tanh, scale=0.5).then_inc(tanh_ready, 1)
                elif name == "TH":
                    act.wait_ge(misc_read, idx + 1)
                    sc.activation(hid_g[:], hid[:], ACT.Gelu).then_inc(gelu_ready, 1)
                elif name == "FE":
                    _, n, fi = arg
                    act.wait_ge(f_norm, 2 * fi + 2)
                    act.dma_start(out[bass.ds(n, 1)].rearrange("a (t p) d -> (a p) t d", p=P), f1).then_inc(stored, 16)

            for k in range(KT):
                act.wait_ge(w_loaded[k], 16)
                sc.copy(w_hi[:, k, :], stage_w[:, k, :]).then_inc(hi_split, 1)
            for n, name in enumerate(("XT0", "XT1", "XTE")):
                step(name, 0, n, "first")
            spread_keys(0, 0)

            def body(it, kind):
                st = state_of(it, kind)
                for q in range(Q_N):
                    g, j = q // 4, q % 4
                    quad = it * Q_N + q
                    for pair, place in ((0, "A"), (1, "B")):
                        copies = [s for s in walk(kind, it, (q, place), st)]
                        early = [s for s in copies if pair == 1 and s[0] in PE_FED]
                        for name, arg, idx in early:
                            step(name, arg, idx, kind)
                        exps(quad, q, pair)
                        if pair == 1:
                            gather_front(quad, q)
                        for name, arg, idx in copies:
                            if (name, arg, idx) not in early:
                                step(name, arg, idx, kind)
                        if pair == 0 and not (kind == "first" and q == 0):
                            copy_transposed(quad - 1, (q - 1) % 2)
                        if place == "A" and j > 0:
                            p = proj_at(g, j - 1, "B")
                            if p and p[1] == "E" and not (kind == "last" and g == 3):
                                spread_keys(it * GROUPS + g + 1, (g + 1) % 2)
                    for name, arg, idx in walk(kind, it, (q, "C"), st):
                        step(name, arg, idx, kind)
                    if kind == "thought" and q == THOUGHT_AT[0][0] - 2:
                        act.wait_ge(x1_stored, NSTORE * 16)
                        act.dma_start(last_x[:], store[P - 1:P, 0, :, (TILES - 1) * D:]).then_inc(tail_x, 16)

            chunks(act, body)
            copy_transposed(NCH * Q_N - 1, 1)
            for name, arg, idx in tail_steps():
                step(name, arg, idx, "tail")
            act.wait_ge(stored, NCH * 16 + 16)

        @block.gpsimd
        def _(pool):
            gp = nc.gpsimd

            def add(stage, par, what):
                k = PJOBS.index(what)
                pool.wait_ge(rope_mul, stage * P_FIRST + k + 1)
                lo, hi = columns(what)
                c, s = rope_c[:, k % 2, 0:hi - lo], rope_s[:, k % 2, 0:hi - lo]
                if what == "K":
                    if not (isinstance(stage, int) and stage < 2):
                        pool.wait_ge(s_done, (stage - 1) * 8)
                    if not (isinstance(stage, int) and stage == 0):
                        pool.wait_ge(k_ready, stage)
                    gp.tensor_tensor(k_ext[:, :], c[:, 0:EXT], s[:, 0:EXT], ALU.add)
                    c, s = c[:, EXT:], s[:, EXT:]
                    dst = k_sb[:, par, 0:3, FRONT + BLK:]
                elif what == "E":
                    dst = k_sb[:, par, 3:, FRONT + BLK:]
                else:
                    dst = q_sb[:, par, what // 2, :, what % 2 * BLK:(what % 2 + 1) * BLK]
                c, s = (a.rearrange("p (u n) -> p u n", n=BLK) for a in (c, s))
                gp.tensor_tensor(dst, c, s, ALU.add).then_inc(rope_add, 1)

            def inverse_root(var, work, eps, ve, ve_n, done):
                gp.tensor_tensor(work[0], var, eps[0:var.shape[0], 0:var.shape[1]], ALU.add).then_inc(ve, 1)
                pool.wait_ge(ve, ve_n)
                gp.tensor_tensor(work[1], work[0], half_pow[0:work[0].shape[0], 0:work[0].shape[1]], ALU.pow).then_inc(done, 1)

            def th_inverse_root(n):
                pool.wait_ge(th_mv, n + 1)
                inverse_root(tmv[:, 1:2], (trs[:, 0:1], trs[:, 1:2]), eps2, th_ve, n + 1, th_rstd)

            def step(name, arg, idx):
                if name == "BN":
                    pool.wait_ge(mv_ready, arg + 1)
                    inverse_root(mv[:, :, 1], (rstd[:, 0, :], rstd[:, 1, :]), eps1, ve_ready, arg + 1, rstd_ready)
                elif name == "TA":
                    th_inverse_root(1)
                elif name == "TD" and (arg - 2) // 3 < STEPS - 1:
                    th_inverse_root(2 + (arg - 2) // 3)
                elif name in FINAL:
                    src, n, fi = arg
                    xs, _, _ = sources(src, n)
                    if name == "FA":
                        pool.wait_ge(f_gated, fi + 2)
                        if src == "S":
                            pool.wait_ge(x1_stored, n * 16 + 16)
                        gp.tensor_tensor(f1, f1, xs, ALU.add).then_inc(f_sum, 1)
                    elif name in ("FB", "FD"):
                        n = 2 * fi + (1 if name == "FB" else 2)
                        pool.wait_ge(f_mv, n)
                        inverse_root(fmv[:, :, 1], (frstd[:, 0, :], frstd[:, 1, :]), eps2 if name == "FB" else eps1, f_ve, n, f_rstd)
                    elif name == "FC":
                        pool.wait_ge(f_norm, 2 * fi + 1)
                        gp.tensor_tensor(f2, f2, out_gamma[:, None, :].broadcast_to([P, TILES, D]), ALU.mult)
                        gp.tensor_tensor(f1, xs, out_beta[:, None, :].broadcast_to([P, TILES, D]), ALU.add).then_inc(f_scaled, 1)
                        pool.wait_ge(f_scaled, fi + 1)
                        gp.tensor_tensor(f2, f2, f1, ALU.add).then_inc(f_added, 1)

            pool.wait_ge(const_set, 1)
            for what in PJOBS:
                add(0, 0, what)

            def body(it, kind):
                st = state_of(it, kind)
                for q in range(Q_N):
                    g, j = q // 4, q % 4
                    for place in "ABC":
                        for name, arg, idx in walk(kind, it, (q, place), st):
                            step(name, arg, idx)
                        p = proj_at(g, j, place)
                        if p and not (kind == "last" and g == 3):
                            add(it * GROUPS + g + 1, (g + 1) % 2, p[1])
                    if kind == "thought" and q == THOUGHT_AT[0][0] - 1:
                        th_inverse_root(0)

            chunks(pool, body)
            for name, arg, idx in tail_steps():
                step(name, arg, idx)


def kernel(**inputs):
    import numpy as np
    import concourse.bacc as bacc
    from concourse.bass_utils import run_bass_kernel_spmd

    a = {k: np.asarray(v) for k, v in inputs.items()}
    import ml_dtypes
    bf = ml_dtypes.bfloat16
    f = np.float32

    def split_rows(w, tiles):
        return np.ascontiguousarray(w.reshape(tiles, P, -1).transpose(1, 0, 2))

    x = a["L0_attn_x"]
    steps = []
    for it in range(NCH):
        b, c = it % BATCH, 1 - it // BATCH
        prev = max(c * CHUNK - BLK, 0)
        steps.append(np.concatenate([x[b, prev:prev + BLK], x[b, :FRONT], x[b, c * CHUNK:(c + 1) * CHUNK]]))
    order = np.concatenate([np.arange(0, P, 2), np.arange(1, P, 2)])
    wq = a["L0_attn_wq"].reshape(D, HEADS, P)[:, :, order].reshape(D, HEADS * P)
    wk = a["L0_attn_wk"].reshape(D, GROUPS, P)[:, :, order].reshape(D, GROUPS * P)
    w_all = split_rows(np.concatenate([wq, wk, a["L0_attn_wv"]], axis=1), KT)
    wo_t = np.ascontiguousarray(a["L0_attn_wo"].reshape(HEADS // 2, 2, DV, D).transpose(0, 2, 1, 3).reshape(P, 2, D))
    inv = (1.0 / 10000.0 ** (np.arange(0, P, 2)[:P // 2].astype(f) / P))
    ang = np.outer(np.arange(SEQ, dtype=f), inv.astype(f))
    cos, sin = np.cos(ang).T.astype(np.float64), np.sin(ang).T.astype(np.float64)
    scale = float(P) ** -0.25
    rope = np.empty((2, P, 2, XW), f)
    for half in range(2):
        c = 1 - half
        prev = max(c * CHUNK - BLK, 0)
        pos = np.concatenate([np.arange(prev, prev + BLK), np.arange(FRONT), np.arange(c * CHUNK, (c + 1) * CHUNK)])
        rope[half, :, 0] = np.concatenate([cos[:, pos], cos[:, pos]]) * scale
        rope[half, :, 1] = np.concatenate([sin[:, pos], -sin[:, pos]]) * scale
    NEG = -1e30
    i, k = np.arange(BLK)[:, None], np.arange(2 * BLK)[None, :]
    std = np.where((k > i) & (k <= i + BLK), 0.0, NEG)
    edge = np.zeros((2, BLK, 2, KEYS))
    edge[:, :, :, FRONT:] = std[:, None, :]
    edge[1, :, 0, :FRONT + BLK] = NEG
    edge[1, :, 1, :FRONT] = np.where(np.arange(FRONT)[None, :] <= i, 0.0, NEG)
    std2, edge2 = np.concatenate([std, std]).astype(bf), np.concatenate([edge, edge], axis=1).astype(bf)
    select = np.zeros((BATCH, BATCH, P), f)
    for b in range(BATCH):
        select[b, b] = 0.5
    vec = lambda names, n: np.ascontiguousarray(np.broadcast_to(np.stack([a["L0_ffn_" + x] for x in names]), (n, len(names), D)))
    arrays = {
        "x_steps": np.stack(steps), "w_all": w_all, "wo_t": wo_t, "gate_t": split_rows(a["L0_ffn_gate_w"], KT),
        "agg_t": split_rows(a["L0_ffn_agg_w"], KT), "bc_t": split_rows(a["L0_ffn_bc_w"], KT),
        "d1_t": split_rows(a["L0_ffn_d1_w"], KT), "d2_t": split_rows(a["L0_ffn_d2_w"], HT),
        "d1b_t": np.ascontiguousarray(a["L0_ffn_d1_b"].reshape(HT, P).T),
        "vec128": vec(["gate_b", "out_gamma", "out_beta"], P),
        "vec4": vec(["in_gamma", "in_beta", "agg_b", "pn_gamma", "pn_beta", "d2_b", "bc_b"], BATCH),
        "rope": rope, "mask_std": std2, "mask_edge": edge2, "ident_bf": np.eye(P).astype(bf), "ident_f": np.eye(P, dtype=f),
        "select": select,
    }
    nc = bacc.Bacc("TRN2", target_bir_lowering=False, num_devices=1)
    args = [nc.dram_tensor(n, v.shape, mybir.dt.from_np(v.dtype), kind="ExternalInput").ap() for n, v in arrays.items()]
    out = nc.dram_tensor("out", (NCH, CHUNK, D), mybir.dt.float32, kind="ExternalOutput").ap()
    build(nc, *args, out)
    r = run_bass_kernel_spmd(nc, [arrays], core_ids=[0])
    got = r.results[0]["out"]
    return np.ascontiguousarray(got.reshape(2, BATCH, CHUNK, D)[::-1].transpose(1, 0, 2, 3).reshape(BATCH, SEQ, D))
```

```python
from contextlib import ExitStack

import concourse.bass as bass
from concourse import mybir
from concourse.alu_op_type import AluOpType as ALU

P = 128
D = 256
KT = D // P
SEQ, BATCH = 1024, 4
CHUNK = 512
NCH = SEQ * BATCH // CHUNK
NSTORE = BATCH
TILES = CHUNK // P
HEADS, GROUPS, REP = 16, 4, 4
DV = D // HEADS
VW = DV + 1
BLK, FRONT = 64, 32
NBLK = CHUNK // BLK
EXT = BLK + FRONT
KSPLIT = EXT + 3 * BLK
XW = EXT + CHUNK
KEYS = FRONT + 2 * BLK
H = 1024
HT = H // P
STEPS = 4
WPART, WV0, WV = (1 + REP) * P, (1 + REP) * P, GROUPS * DV
WALL = GROUPS * WPART + WV
WSTART = [0] + [WV + g * WPART for g in range(1, GROUPS)]
WEND = [WV + (g + 1) * WPART for g in range(GROUPS)]
EPS1, EPS2 = 1e-5, 1e-6

EPILOGUE = {(2, "A"): ["OT0"], (2, "B"): ["OT1"], (3, "A"): ["OP0"], (3, "B"): ["OP1", "BN0"], (3, "C"): ["BN1"], (4, "A"): ["NM0"],
            (4, "B"): ["NM1"], (5, "A"): ["X1T0"], (5, "B"): ["X1T1"], (6, "A"): ["G0"], (6, "B"): ["G1"]}
PREPARE = {(11, "B"): ["XT0"], (12, "A"): ["XT1"], (12, "B"): ["XTE"]}
THOUGHT = [("TX", 0, (5, "B")), ("TM", 0, (5, "C")), ("TN", 0, (6, "A")), ("TA", 0, (6, "B")), ("TM", 1, (6, "C"))]
for n in range(STEPS):
    THOUGHT += [("TT", n, (7 + 2 * n, "A")), ("TH", n, (7 + 2 * n, "B")), ("TD", n, (8 + 2 * n, "A"))]
    THOUGHT += [("TM", n + 2, (8 + 2 * n, "B"))] if n < STEPS - 1 else []
THOUGHT += [("TU", 0, (14, "B")), ("TB0", 0, (15, "A")), ("TB1", 0, (15, "B"))]
PE_FED = ("OT0", "OT1", "X1T0", "X1T1", "XT0", "XT1", "XTE")
FINAL = ["FA0", "FA1", "FX0", "FB0", "FB1", "FX1", "FC0", "FC1", "FG0", "FG1", None, "FD0", "FD1", None, None, "FE0", "FE1"]
FINAL_S, FINAL_E, FINAL_S3 = 0, 7, 12
MISC_JOBS = {"V", "OT0", "OT1", "OP0", "OP1", "X1T0", "X1T1", "G0", "G1", "XT0", "XT1", "XTE", "TN", "TA", "TT", "TH", "TD", "TU", "TB0", "TB1"}
N_EPI, N_PREP, N_THOUGHT = 8, 3, sum(name in MISC_JOBS for name, _, _ in THOUGHT)
PROJECT = {(0, "A"): "K", (0, "B"): "E", (1, "A"): 0, (1, "B"): 1, (2, "A"): 2, (3, "A"): 3}
PROJECT_LAST = {(1, "A"): "K", (1, "B"): "E", (2, "A"): 0, (2, "B"): 1, (3, "A"): 2, (3, "B"): 3}
PJOBS = ["K", "E", 0, 1, 2, 3]



def plan(it, kind):
    steps = {(1, "A"): [("V", it)]}

    def add(at, names, arg):
        steps.setdefault(at, []).extend((n, arg) for n in names)

    if kind != "first":
        for at, names in EPILOGUE.items():
            add(at, names, it - 1)
    if kind == "thought":
        for name, n, at in THOUGHT:
            add(at, [name], n)
    if kind != "last":
        for at, names in PREPARE.items():
            add(at, names, it + 1)
    if kind in ("final", "last"):
        starts = [(FINAL_S, ("S", it - 5, (it - 5) * 2)), (FINAL_E, ("E", it - 1, (it - 5) * 2 + 1))]
        if kind == "last":
            starts.append((FINAL_S3, ("S", 3, 6)))
        for slot, arg in starts:
            for n, name in enumerate(FINAL):
                at = (slot + n // 3, "ABC"[n % 3])
                if name and at[0] < 16:
                    add(at, [name], arg)
    if kind == "last":
        add((15, "B"), ["OT0"], it)
        add((15, "C"), ["OP0"], it)
    return steps


def misc_base(it):
    if isinstance(it, int) and it == 0:
        return N_PREP
    return it * (1 + N_EPI + N_PREP) - N_EPI + N_PREP


def build(nc, x_steps, w_all, wo_t, gate_t, agg_t, bc_t, d1_t, d2_t, d1b_t, vec128, vec4, rope, mask_std,
          mask_edge, ident_bf, ident_f, out):
    f32, f32r, bf16 = mybir.dt.float32, mybir.dt.float32r, mybir.dt.bfloat16
    ACT = mybir.ActivationFunctionType
    AX = mybir.AxisListType
    ctx = ExitStack()
    with ctx:
        sb = lambda n, s, d=f32: ctx.enter_context(nc.sbuf_tensor(n, s, d))
        ps = lambda n, s: ctx.enter_context(nc.psum_tensor(n, s, f32))
        sem = lambda n: ctx.enter_context(nc.semaphore(n))

        w_hi, w_lo = sb("w_hi", [P, KT, WALL], f32r), sb("w_lo", [P, KT, WALL], f32r)
        wo_sb, gate_w = sb("wo_sb", [P, KT, D]), sb("gate_w", [P, KT, D])
        agg_w, bc_w = sb("agg_w", [P, KT, D]), sb("bc_w", [P, KT, D])
        d1_w, d2_w, d1_b = sb("d1_w", [P, KT, H]), sb("d2_w", [P, HT, D]), sb("d1_b", [P, HT])
        v128, v4 = sb("v128", [P, 4, D]), sb("v4", [BATCH, 6, D])
        gate_b, out_gamma, out_beta, bc_b = (v128[:, n, :] for n in range(4))
        in_gamma, in_beta, agg_b, pn_gamma, pn_beta, d2_b = (v4[:, n, :] for n in range(6))
        rope_sb = sb("rope_sb", [P, 2, XW])
        std_sb, edge_sb = sb("std_sb", [P, 2 * BLK], bf16), sb("edge_sb", [P, 2, KEYS], bf16)
        id_bf, id_f = sb("id_bf", [P, P], bf16), sb("id_f", [P, P])
        x_in = sb("x_in", [P, 1 + TILES, D])
        x_hi, x_lo = sb("x_hi", [P, KT, XW], f32r), sb("x_lo", [P, KT, XW], f32r)
        rope_c, rope_s = sb("rope_c", [P, 2, CHUNK]), sb("rope_s", [P, 2, CHUNK])
        q_sb = sb("q_sb", [P, 2, 2, NBLK, P])
        k_ext, k_sb = sb("k_ext", [P, EXT]), sb("k_sb", [P, 2, NBLK, KEYS])
        v_sb, vf_sb = sb("v_sb", [P, NBLK, GROUPS, VW]), sb("vf_sb", [P, GROUPS, 4 * VW])
        neg_max = sb("neg_max", [P, 4, 2])
        prob = sb("prob", [P, 2, 4, KEYS])
        prob_f = sb("prob_f", [P, 2, 4, FRONT])
        prob_t = sb("prob_t", [P, 2, 5 * P])
        rcp, o_sb = sb("rcp", [P, 2, 4]), sb("o_sb", [P, NBLK, P])
        e_t = sb("e_t", [P, KT, CHUNK])
        y, x1, z = sb("y", [P, TILES, D]), sb("x1", [P, TILES, D]), sb("z", [P, TILES, D])
        store = sb("store", [P, 2, NSTORE, TILES * D])
        stats, mv = sb("stats", [P, TILES, 6]), sb("mv", [P, TILES, 2])
        rstd, half_pow = sb("rstd", [P, 3, TILES]), sb("half_pow", [P, TILES])
        minus_one = sb("minus_one", [P, TILES])
        eps1, eps2 = sb("eps1", [P, TILES]), sb("eps2", [P, TILES])
        carry = sb("carry", [1, 1])
        f1 = d1_w[:, 0, :].rearrange("p (t d) -> p t d", t=TILES)
        f2 = d1_w[:, 1, :].rearrange("p (t d) -> p t d", t=TILES)
        f_x, f_o = d2_w[:, 0:TILES, :], d2_w[:, TILES:2 * TILES, :]
        fstats, fmv = sb("fstats", [P, TILES, 6]), sb("fmv", [P, TILES, 2])
        frstd = [sb(f"frstd{n}", [P, 3, TILES]) for n in range(2)]
        bc_sb = sb("bc_sb", [P, BATCH, D])
        last_x, th = sb("last_x", [BATCH, D]), sb("th", [BATCH, D])
        tn, tst, tmv, trs = sb("tn", [BATCH, D]), sb("tst", [BATCH, 6]), sb("tmv", [BATCH, 2]), sb("trs", [BATCH, 2])
        t_t, hid, hid_g = sb("t_t", [P, KT, BATCH]), sb("hid", [P, HT, BATCH]), sb("hid_g", [P, HT, BATCH])
        stage_w = store[:, :, :, :].rearrange("p a n d -> p (a n d)")[:, 0:KT * WALL].rearrange("p (k n) -> p k n", k=KT)

        pj = [ps(f"pj{n}", [P, 512]) for n in range(2)]
        s_ps = [ps(f"s_ps{n}", [P, 512]) for n in range(2)]
        pt_ps, pf_ps = ps("pt_ps", [P, 512]), ps("pf_ps", [P, 512])
        pv_ps, misc = ps("pv_ps", [P, 512]), ps("misc", [P, 512])
        misc_bank, first_banks = misc, [misc, s_ps[0], s_ps[1]]
        v_ps = [misc[:, t * GROUPS * DV:(t + 1) * GROUPS * DV] for t in range(TILES + 1)]

        w_loaded, id_loaded, c_loaded, ffn_loaded = [sem(f"w_loaded{g}") for g in range(GROUPS)], sem("id_loaded"), sem("c_loaded"), sem("ffn_loaded")
        x_loaded, rope_loaded, edge_loaded, res_loaded = sem("x_loaded"), sem("rope_loaded"), sem("edge_loaded"), sem("res_loaded")
        const_step, const_set, hi_split, w_split = sem("const_step"), sem("const_set"), sem("hi_split"), [sem(f"w_split{g}") for g in range(GROUPS)]
        proj_done, rope_mul, rope_add, k_ready = sem("proj_done"), sem("rope_mul"), sem("rope_add"), sem("k_ready")
        s_done, max_done, exp_done = sem("s_done"), sem("max_done"), sem("exp_done")
        t_done, pt_ready, pv_done, rcp_done, o_ready, front_ready = sem("t_done"), sem("pt_ready"), sem("pv_done"), sem("rcp_done"), sem("o_ready"), sem("front_ready")
        misc_done, misc_read, xhi_ready = sem("misc_done"), sem("misc_read"), sem("xhi_ready")
        bn_done, mv_ready, ve_ready, rstd_ready, x1_ready = sem("bn_done"), sem("mv_ready"), sem("ve_ready"), sem("rstd_ready"), sem("x1_ready")
        tanh_ready, x1_stored, tail_x = sem("tanh_ready"), sem("x1_stored"), sem("tail_x")
        f_gated, f_sum, f_bn, f_mv, f_ve, f_rstd = sem("f_gated"), sem("f_sum"), sem("f_bn"), sem("f_mv"), sem("f_ve"), sem("f_rstd")
        f_norm, f_scaled, f_added, stored = sem("f_norm"), sem("f_scaled"), sem("f_added"), sem("stored")
        f_beta, f_out = sem("f_beta"), sem("f_out")
        th_rows, th_mv, th_ve, th_rstd = sem("th_rows"), sem("th_mv"), sem("th_ve"), sem("th_rstd")
        th_link, gelu_ready = sem("th_link"), sem("gelu_ready")

        S_N, Q_N, P_N = 32, 16, 24
        P_FIRST = len(PJOBS)

        def thought_jobs(kind):
            return N_THOUGHT if kind in ("final", "last", "tail") else 0

        def walk(kind, it, place, state):
            for name, arg in state["steps"].get(place, []):
                idx = state["base"] + state["n"]
                if name in MISC_JOBS:
                    state["n"] += 1
                yield name, arg, idx

        def state_of(it, kind):
            return {"steps": plan(it, kind), "base": misc_base(it) + thought_jobs(kind), "n": 0}

        def columns(what):
            return {"K": (0, KSPLIT), "E": (KSPLIT, XW)}.get(what, (EXT, XW))

        def proj_at(g, j, place):
            table = PROJECT_LAST if g == 3 else PROJECT
            what = table.get((j, place))
            return None if what is None else (6 * g + PJOBS.index(what), what)

        def chunks(eng, body):
            body(0, "first")
            with eng.Fori(1, 4) as it:
                body(it, "store")
            body(4, "thought")
            with eng.Fori(5, 7) as it:
                body(it, "final")
            body(7, "last")

        tail_plan = [(n, 7) for n in ("BN0", "OT1", "NM0", "OP1", "X1T0", "BN1", "G0", "NM1", "X1T1")]
        tail_plan += [(n, ("S", 3, 6)) for n in ("FD1", "FE0", "FE1")]
        tail_plan += [(n, 7 if n[0] == "G" else ("E", 7, 7)) for n in (
            "FX0", "FA0", "G1", "FB0", "FX1", "FA1", "FC0", "FB1", "FG0", "FC1", "FD0", "FG1", "FE0", "FD1", "FE1")]

        def tail_steps():
            idx = misc_base(7) + N_THOUGHT + 1 + N_EPI + 2
            for name, arg in tail_plan:
                yield name, arg, idx
                if name in MISC_JOBS:
                    idx += 1

        thought_over = misc_base(5) + N_THOUGHT

        def sources(src, n):
            if src == "S":
                at = bass.ds(n, 1)
                xs, ts = (store[:, k, at, :].rearrange("p a (t d) -> p (a t) d", t=TILES) for k in range(2))
                return xs, ts, bc_sb[:, at, :]
            return x1[:, :, :], z[:, :, :], bc_sb[:, bass.ds(n - NSTORE, 1), :]

        block = ctx.enter_context(nc.Block())

        @block.sync
        def _(sp):
            def load_x(n):
                sp.dma_start(x_in[0:EXT, 0, :], x_steps[bass.ds(n, 1), 0:EXT, :].rearrange("a p d -> (a p) d")).then_inc(x_loaded, 16)
                sp.dma_start(x_in[:, 1:, :], x_steps[bass.ds(n, 1), EXT:XW, :].rearrange("a (t p) d -> (a p) t d", p=P)).then_inc(x_loaded, 16)

            def load_rope(n, half):
                sp.dma_start(rope_sb[:], rope[bass.ds(half, 1)].rearrange("a p c n -> (a p) c n")).then_inc(rope_loaded, 16)

            def load_edge(half):
                sp.dma_start(edge_sb[:], mask_edge[bass.ds(half, 1)].rearrange("a p u n -> (a p) u n")).then_inc(edge_loaded, 16)

            def load_w(g):
                sp.dma_start(stage_w[:, :, WSTART[g]:WEND[g]], w_all[:, :, WSTART[g]:WEND[g]]).then_inc(w_loaded[g], 16)

            sp.dma_start(id_f[:], ident_f).then_inc(id_loaded, 16)
            load_x(0)
            load_w(0)
            load_rope(0, 0)
            sp.dma_start(id_bf[:], ident_bf).then_inc(c_loaded, 16)
            sp.dma_start(std_sb[:], mask_std).then_inc(c_loaded, 16)
            load_edge(0)
            for g in range(1, GROUPS):
                load_w(g)
            for dst, src in ((wo_sb, wo_t), (gate_w, gate_t), (agg_w, agg_t), (bc_w, bc_t), (d1_w, d1_t),
                             (d2_w, d2_t), (d1_b, d1b_t), (v128, vec128), (v4, vec4)):
                sp.dma_start(dst[:], src).then_inc(ffn_loaded, 16)

            def store_x1(n):
                sp.dma_start(store[:, 0, bass.ds(n, 1), :].rearrange("p a d -> p (a d)"), x1[:, :, :].rearrange("p t d -> p (t d)")).then_inc(x1_stored, 16)

            def output(n, fi):
                for a in range(2):
                    sp.wait_ge(f_out, 2 * fi + a + 2)
                    sp.dma_start(out[bass.ds(n, 1), a * 2 * P:(a + 1) * 2 * P].rearrange("a (t p) d -> (a p) t d", p=P),
                                 f_o[:, 2 * a:2 * a + 2, :]).then_inc(stored, 16)

            def body(it, kind):
                if kind != "last":
                    sp.wait_ge(misc_done, misc_base(it) + thought_jobs(kind))
                    load_x(it + 1)
                if kind != "first":
                    sp.wait_ge(x1_ready, it * 2)
                if kind in ("store", "thought"):
                    store_x1(it - 1)
                if kind == "thought":
                    sp.wait_ge(x1_stored, (BATCH - 1) * 16)
                    sp.dma_start(last_x[0:BATCH - 1], store[P - 1:P, 0, 0:BATCH - 1, (TILES - 1) * D:]).then_inc(tail_x, 16)
                    sp.dma_start(last_x[BATCH - 1:], x1[P - 1:P, TILES - 1, :]).then_inc(tail_x, 16)
                sp.dma_start(y[:], x_steps[bass.ds(it, 1), EXT:XW, :].rearrange("a (t p) d -> (a p) t d", p=P)).then_inc(res_loaded, 16)
                if kind in ("final", "last"):
                    output(it - 5, (it - 5) * 2)
                if kind != "last":
                    half = {"first": 0, "thought": 1, "final": 1}.get(kind)
                    nxt = half if half is not None else (it + 1) // NSTORE
                    sp.wait_ge(rope_mul, it * P_N + P_N)
                    load_rope(it + 1, nxt)
                if kind in ("final", "last"):
                    output(it - 1, (it - 5) * 2 + 1)
                if kind != "last":
                    sp.wait_ge(s_done, it * S_N + 3 * 8 + 2)
                    load_edge(nxt)

            chunks(sp, body)
            output(3, 6)
            output(7, 7)
            sp.wait_ge(stored, NCH * 32 + 16)

        @block.tensor
        def _(pe):
            mm = nc.tensor.matmul

            def split_mm(o, w, x):
                for k in range(KT):
                    for n, (a, b) in enumerate(((w_hi, x_hi), (w_hi, x_lo), (w_lo, x_hi))):
                        last = mm(o, w(a, k), x(b, k), start=(k == 0 and n == 0), stop=(k == KT - 1 and n == 2))
                return last

            def project(idx, g, what):
                if not (isinstance(idx, int) and idx < 2):
                    pe.wait_ge(rope_mul, idx - 1)
                bank = pj[PJOBS.index(what) % 2]
                col = WSTART[g] + (0 if what in ("K", "E") else (1 + what) * P)
                lo, hi = columns(what)
                split_mm(bank[:, 0:hi - lo], lambda a, k: a[:, k, col:col + P],
                         lambda b, k: b[:, k, lo:hi]).then_inc(proj_done, 1)

            def scores(it, g, j, pair):
                pe.wait_ge(rope_add, it * P_N + g * P_FIRST + 2 * pair + 4)
                if pair == 0:
                    pe.wait_ge(k_ready, it * GROUPS + g + 1)
                if not (isinstance(it, int) and it == 0 and g == 0 and j == 0):
                    pe.wait_ge(exp_done, it * S_N + g * 8 + 2 * j + pair - 1)
                if j == 0 and pair == 0 and g == 0:
                    pe.wait_ge(edge_loaded, it * 16 + 16)
                bank = s_ps[pair][:, 0:2 * KEYS].rearrange("p (u n) -> p u n", u=2)
                for u in range(2):
                    blk = 2 * j + u
                    mm(bank[:, u, :], q_sb[:, g % 2, pair, blk, :],
                       k_sb[:, g % 2, blk, :], start=(u == 0), stop=False)
                if j == 0:
                    last = mm(bank, id_bf[:], edge_sb[:], start=False, stop=True)
                else:
                    last = mm(bank[:, :, FRONT:], id_bf[:], std_sb[:, None, :].broadcast_to([P, 2, 2 * BLK]), start=False, stop=True)
                last.then_inc(s_done, 1)

            def transposes(quad, par):
                pe.wait_ge(front_ready, quad + 1)
                if not (isinstance(quad, int) and quad == 0):
                    pe.wait_ge(pt_ready, quad)
                for n in range(4):
                    nc.tensor.transpose(pt_ps[:, n * P:(n + 1) * P], prob[:, par, n, FRONT:], id_f[:])
                nc.tensor.transpose(pf_ps[:, 0:P], prob_f[:, par, :, :].rearrange("p n k -> p (n k)"), id_f[:]).then_inc(t_done, 1)

            def values(quad, par, g, j):
                pe.wait_ge(pt_ready, quad + 1)
                if not (isinstance(quad, int) and quad == 0):
                    pe.wait_ge(o_ready, quad)
                mm(pv_ps[:, 0:4 * VW], prob_t[:, par, 4 * P:], vf_sb[:, g, :], start=True, stop=False)
                for n in range(4):
                    last = mm(pv_ps[:, n * VW:(n + 1) * VW], prob_t[:, par, n * P:(n + 1) * P],
                              v_sb[:, 2 * j + n % 2, g, :], start=False, stop=(n == 3))
                last.then_inc(pv_done, 1)

            def to_misc(idx):
                if not (isinstance(idx, int) and idx == 0):
                    pe.wait_ge(misc_read, idx)

            def step(name, arg, idx, misc=misc):
                if name not in MISC_JOBS:
                    return
                if misc is misc_bank:
                    to_misc(idx)
                if name == "V":
                    for t in range(TILES + 1):
                        at = EXT + t * P if t < TILES else 0
                        last = split_mm(v_ps[t], lambda a, k: x_hi[:, k, at:at + P] if a is w_hi else x_lo[:, k, at:at + P],
                                        lambda b, k: (w_hi if b is x_hi else w_lo)[:, k, WV0:WV0 + WV])
                elif name in ("XT0", "XT1", "XTE"):
                    if name == "XT0":
                        pe.wait_ge(x_loaded, arg * 32 + 32)
                    if name == "XTE":
                        for k in range(KT):
                            last = nc.tensor.transpose(misc[:, k * EXT:(k + 1) * EXT], x_in[0:EXT, 0, k * P:(k + 1) * P], id_f[0:EXT, 0:EXT])
                    else:
                        k = int(name[2])
                        for t in range(TILES):
                            last = nc.tensor.transpose(misc[:, t * P:(t + 1) * P], x_in[:, 1 + t, k * P:(k + 1) * P], id_f[:])
                elif name in ("OT0", "OT1"):
                    pe.wait_ge(o_ready, arg * Q_N + Q_N - 2 + 2 * int(name[2]))
                    for u in range(4):
                        last = nc.tensor.transpose(misc[:, u * P:(u + 1) * P], o_sb[:, 4 * int(name[2]) + u, :], id_f[:])
                elif name in ("OP0", "OP1", "G0", "G1"):
                    if name == "OP0":
                        pe.wait_ge(ffn_loaded, 144)
                    a, w = int(name[-1]), wo_sb if name[0] == "O" else gate_w
                    for t in range(2):
                        for k in range(KT):
                            last = mm(misc[:, t * D:(t + 1) * D], e_t[:, k, (2 * a + t) * P:(2 * a + t + 1) * P], w[:, k, :],
                                      start=(k == 0), stop=(k == KT - 1))
                elif name in ("X1T0", "X1T1"):
                    a = int(name[3])
                    pe.wait_ge(x1_ready, arg * 2 + a + 1)
                    for k in range(KT):
                        for t in range(2):
                            last = nc.tensor.transpose(misc[:, (2 * k + t) * P:(2 * k + t + 1) * P], x1[:, 2 * a + t, k * P:(k + 1) * P], id_f[:])
                elif name in ("TN", "TT", "TU"):
                    pe.wait_ge(th_rows, {"TN": 1, "TU": 2 + STEPS}.get(name, 2 + arg))
                    rows = th if name == "TU" else tn
                    for k in range(KT):
                        last = nc.tensor.transpose(misc[:, k * BATCH:(k + 1) * BATCH], rows[:, k * P:(k + 1) * P], id_f[0:BATCH, 0:BATCH])
                elif name == "TA":
                    for k in range(KT):
                        last = mm(misc[0:BATCH, 0:D], t_t[:, k, :], agg_w[:, k, :], start=(k == 0), stop=(k == KT - 1))
                elif name == "TH":
                    for m in range(HT):
                        for k in range(KT):
                            last = mm(misc[:, m * BATCH:(m + 1) * BATCH], d1_w[:, k, m * P:(m + 1) * P], t_t[:, k, :], start=(k == 0), stop=(k == KT - 1))
                elif name == "TD":
                    pe.wait_ge(gelu_ready, arg + 1)
                    for m in range(HT):
                        last = mm(misc[0:BATCH, 0:D], hid_g[:, m, :], d2_w[:, m, :], start=(m == 0), stop=(m == HT - 1))
                else:
                    for b in range(2):
                        for k in range(KT):
                            row = t_t[:, k, 2 * int(name[2]) + b:2 * int(name[2]) + b + 1].broadcast_to([P, P])
                            last = mm(misc[:, b * D:(b + 1) * D], row, bc_w[:, k, :], start=(k == 0), stop=(k == KT - 1))
                last.then_inc(misc_done, 1)

            pe.wait_ge(id_loaded, 16)
            for n, name in enumerate(("XT0", "XT1", "XTE")):
                step(name, 0, n, first_banks[n])
            pe.wait_ge(misc_read, N_PREP)
            pe.wait_ge(w_split[0], 1)
            for n, what in enumerate(PJOBS):
                project(n, 0, what)
            pe.wait_ge(c_loaded, 32)
            pe.wait_ge(const_set, 1)

            def body(it, kind):
                st = state_of(it, kind)
                x_read = None
                for q in range(Q_N):
                    g, j = q // 4, q % 4
                    quad = it * Q_N + q
                    for pair, place in ((0, "A"), (1, "B")):
                        scores(it, g, j, pair)
                        if pair == 0 and (kind != "first" or q >= 2):
                            if q == 2:
                                pe.wait_ge(misc_read, st["base"] + 1)
                            values(quad - 2, q % 2, (q - 2) % Q_N // 4, (q - 2) % 4)
                        for name, arg, idx in walk(kind, it, (q, place), st):
                            step(name, arg, idx)
                            if name == "XTE":
                                x_read = idx + 1
                        p = proj_at(g, j, place)
                        if p and not (kind == "last" and g == 3):
                            if p[0] == 18:
                                pe.wait_ge(misc_read, x_read)
                            if kind == "first" and p[1] == "K" and g < GROUPS - 1:
                                pe.wait_ge(w_split[g + 1], 1)
                            project(P_FIRST + it * P_N + p[0], (g + 1) % 4, p[1])
                        if pair == 0 and (kind != "first" or q >= 1):
                            transposes(quad - 1, (q - 1) % 2)
                    for name, arg, idx in walk(kind, it, (q, "C"), st):
                        step(name, arg, idx)
                        if name == "XTE":
                            x_read = idx + 1

            chunks(pe, body)
            values(NCH * Q_N - 2, 0, 3, 2)
            transposes(NCH * Q_N - 1, 1)
            values(NCH * Q_N - 1, 1, 3, 3)
            for name, arg, idx in tail_steps():
                step(name, arg, idx)

        @block.vector
        def _(dve):
            v = nc.vector

            def rotate(idx, what):
                dve.wait_ge(proj_done, idx + 1)
                if not (isinstance(idx, int) and idx < 2):
                    dve.wait_ge(rope_add, idx - 1)
                par = PJOBS.index(what) % 2
                lo, hi = columns(what)
                n, half = hi - lo, P // 2
                v.tensor_tensor(rope_c[:, par, 0:n], pj[par][:, 0:n], rope_sb[:, 0, lo:hi], ALU.mult)
                v.tensor_tensor(rope_s[half:P, par, 0:n], pj[par][0:half, 0:n], rope_sb[0:half, 1, lo:hi], ALU.mult)
                v.tensor_tensor(rope_s[0:half, par, 0:n], pj[par][half:P, 0:n], rope_sb[half:P, 1, lo:hi], ALU.mult).then_inc(rope_mul, 1)

            def row_max(idx, pair, slot):
                dve.wait_ge(s_done, idx + 1)
                v.tensor_reduce(out=neg_max[:, slot, :], in_=s_ps[pair][:, 0:2 * KEYS].rearrange("p (u n) -> p u n", u=2),
                                axis=AX.X, op=ALU.max, negate=True).then_inc(max_done, 1)

            def normalize(quad, par):
                dve.wait_ge(pv_done, quad + 1)
                units = pv_ps[:, 0:4 * VW].rearrange("p (n e) -> p n e", e=VW)
                v.reciprocal(rcp[:, par, :], units[:, :, DV]).then_inc(rcp_done, 1)

            def normalize_out(quad, par, g, j):
                dve.wait_ge(rcp_done, quad + 1)
                units = pv_ps[:, 0:4 * VW].rearrange("p (r u e) -> p r u e", r=2, e=VW)
                dst = o_sb[:, 2 * j:2 * j + 2, g * 2 * DV:(g + 1) * 2 * DV].rearrange("p u (r d) -> p r u d", r=2)
                v.tensor_tensor(dst, units[:, :, :, 0:DV], rcp[:, par, :].rearrange("p (r u) -> p r u", r=2)[:, :, :, None].broadcast_to([P, 2, 2, DV]),
                                ALU.mult).then_inc(o_ready, 1)

            def statistics(src, a, st, m, link, n, done):
                for t in (2 * a, 2 * a + 1):
                    last = v.bn_stats(st[:, t, :], src[:, t, :])
                last.then_inc(link, 1)
                dve.wait_ge(link, n + 1)
                v.memset(carry[:], 0.0)
                for t in (2 * a, 2 * a + 1):
                    last = v.bn_aggr(m[:, t, :], st[:, t, :])
                last.then_inc(done, 1)

            def th_norm(rows, gamma, n):
                v.bn_stats(tst[:], rows).then_inc(th_link, 1)
                chain()
                v.bn_aggr(tmv[:], tst[:]).then_inc(th_mv, 1)
                dve.wait_ge(th_mv, n + 1)
                v.scalar_tensor_tensor(out=tn[:], in0=rows, scalar=tmv[:, 0:1], in1=gamma, op0=ALU.subtract, op1=ALU.mult).then_inc(th_link, 1)

            links = [0]

            def chain():
                links[0] += 1
                dve.wait_ge(th_link, links[0])

            def step(name, arg, idx, misc=misc):
                if name in MISC_JOBS and name not in ("OT0", "OT1", "X1T0", "X1T1"):
                    dve.wait_ge(misc_done, idx + 1)
                if name == "V":
                    if not (isinstance(arg, int) and arg == 0):
                        dve.wait_ge(pv_done, arg * Q_N)
                    else:
                        dve.wait_ge(const_set, 1)
                    half, own = P // 2, misc[:, 0:TILES * GROUPS * DV].rearrange("p (t g d) -> p t g d", t=TILES, g=GROUPS)
                    ext = v_ps[TILES].rearrange("p (g d) -> p g d", g=GROUPS)
                    v.tensor_copy(v_sb[:, 1::2, :, 0:DV], own)
                    v.tensor_copy(v_sb[half:P, 0::2, :, 0:DV], own[0:half])
                    v.tensor_copy(v_sb[0:half, 2::2, :, 0:DV], own[half:P, 0:TILES - 1])
                    v.tensor_copy(v_sb[0:half, 0, :, 0:DV], ext[0:half])
                    for n in range(4):
                        last = v.tensor_copy(vf_sb[n * FRONT:(n + 1) * FRONT, :, n * VW:n * VW + DV], ext[BLK:EXT])
                    last.then_inc(misc_read, 1)
                elif name in ("XT0", "XT1", "XTE"):
                    dve.wait_ge(xhi_ready, arg * 3 + ("XT0", "XT1", "XTE").index(name) + 1)
                    if name == "XTE":
                        dst, hi, src = x_lo[:, :, 0:EXT], x_hi[:, :, 0:EXT], misc[:, 0:KT * EXT].rearrange("p (k n) -> p k n", k=KT)
                    else:
                        k = int(name[2])
                        dst, hi, src = x_lo[:, k, EXT:], x_hi[:, k, EXT:], misc[:, :]
                    v.tensor_tensor(dst, src, hi.bitcast(f32), ALU.subtract).then_inc(misc_read, 1)
                elif name in ("OP0", "OP1"):
                    a = int(name[2])
                    if a == 0:
                        dve.wait_ge(res_loaded, arg * 16 + 16)
                    v.tensor_tensor(y[:, 2 * a:2 * a + 2, :], misc[:, :].rearrange("p (t d) -> p t d", t=2), y[:, 2 * a:2 * a + 2, :], ALU.add).then_inc(misc_read, 1)
                    last_res[a] = idx + 1
                elif name in ("BN0", "BN1"):
                    a = int(name[2])
                    dve.wait_ge(misc_read, last_res[a])
                    statistics(y, a, stats, mv, bn_done, arg * 2 + a, mv_ready)
                elif name in ("G0", "G1"):
                    a = int(name[1])
                    if a == 0:
                        free_z(arg)
                    v.tensor_tensor(z[:, 2 * a:2 * a + 2, :], misc[:, :].rearrange("p (t d) -> p t d", t=2),
                                    gate_b[:, None, :].broadcast_to([P, 2, D]), ALU.add).then_inc(misc_read, 1)
                elif name[0] == "F":
                    final(name, *arg)
                elif name[0] == "T":
                    thought(name, arg, idx)

            last_res = [0, 0]
            state = {"kind": None}

            def free_z(arg):
                if isinstance(arg, int) and arg == 0:
                    return
                dve.wait_ge(tanh_ready, arg * 2)
                if state["kind"] not in ("store", "thought"):
                    dve.wait_ge(f_gated, (arg - NSTORE) * 4 + 1)

            def final(name, src, n, fi):
                xs, ts, b = sources(src, n)
                if name[1] not in "ABGD":
                    return
                a = int(name[2])
                tiles = slice(2 * a, 2 * a + 2)
                if name[1] == "A":
                    dve.wait_ge(tanh_ready, n * 2 + (a + 1 if src == "E" else 2))
                    dve.wait_ge(misc_read, thought_over)
                    v.scalar_tensor_tensor(out=f1[:, tiles, :], in0=ts[:, tiles, :], scalar=1.0, in1=b.broadcast_to([P, 2, D]), op0=ALU.add, op1=ALU.mult).then_inc(f_gated, 1)
                elif name[1] == "G":
                    dve.wait_ge(f_norm, 2 * fi + a + 1)
                    v.tensor_tensor(f2[:, tiles, :], f2[:, tiles, :], out_gamma[:, None, :].broadcast_to([P, 2, D]), ALU.mult).then_inc(f_scaled, 1)
                elif name[1] == "B":
                    dve.wait_ge(f_sum, 2 * fi + a + 1)
                    statistics(f1, a, fstats, fmv, f_bn, 4 * fi + a, f_mv)
                else:
                    dve.wait_ge(f_added, 2 * fi + a + 2)
                    statistics(f2, a, fstats, fmv, f_bn, 4 * fi + 2 + a, f_mv)

            def thought(name, n, idx):
                rows = misc[0:BATCH, 0:D]
                if name == "TX":
                    dve.wait_ge(ffn_loaded, 144)
                    v.tensor_scalar(out=bc_b, in0=bc_b, scalar1=0.5, scalar2=None, op0=ALU.mult).then_inc(th_link, 1)
                    chain()
                    dve.wait_ge(tail_x, 32)
                    th_norm(last_x[:], in_gamma, 0)
                elif name == "TM":
                    chain()
                    dve.wait_ge(th_rstd, n + 1)
                    v.scalar_tensor_tensor(out=tn[:], in0=tn[:], scalar=trs[:, 1:2], in1=in_beta if n == 0 else pn_beta, op0=ALU.mult, op1=ALU.add).then_inc(th_rows, 1)
                elif name in ("TN", "TT", "TU"):
                    v.tensor_copy(t_t[:, :, :], misc[:, 0:KT * BATCH].rearrange("p (k b) -> p k b", k=KT)).then_inc(misc_read, 1)
                elif name == "TA":
                    v.tensor_tensor(th[:], rows, agg_b, ALU.add).then_inc(misc_read, 1)
                    dve.wait_ge(misc_read, idx + 1)
                    th_norm(th[:], pn_gamma, 1)
                elif name == "TH":
                    v.tensor_tensor(hid[:], misc[:, 0:HT * BATCH].rearrange("p (m b) -> p m b", m=HT), d1_b[:, :, None].broadcast_to([P, HT, BATCH]), ALU.add).then_inc(misc_read, 1)
                elif name == "TD":
                    v.tensor_tensor(tn[:], rows, d2_b, ALU.add).then_inc(misc_read, 1)
                    dve.wait_ge(misc_read, idx + 1)
                    last = v.tensor_tensor(th[:], th[:], tn[:], ALU.add)
                    if n < STEPS - 1:
                        last.then_inc(th_link, 1)
                        chain()
                        th_norm(th[:], pn_gamma, 2 + n)
                    else:
                        last.then_inc(th_rows, 1)
                else:
                    a = int(name[2])
                    v.scalar_tensor_tensor(out=bc_sb[:, 2 * a:2 * a + 2, :], in0=misc[:, :].rearrange("p (b d) -> p b d", b=2), scalar=0.5,
                                           in1=bc_b[:, None, :].broadcast_to([P, 2, D]), op0=ALU.mult, op1=ALU.add).then_inc(misc_read, 1)

            v.memset(vf_sb[:], 0.0).then_inc(const_step, 1)
            dve.wait_ge(const_step, 1)
            for n in range(4):
                v.memset(vf_sb[n * FRONT:(n + 1) * FRONT, :, n * VW + DV:(n + 1) * VW], 1.0)
            v.memset(eps1[:], EPS1)
            v.memset(eps2[:], EPS2)
            v.memset(frstd[0][:], 0.0).then_inc(f_gated, 1)
            v.memset(half_pow[:], -0.5).then_inc(f_added, 1)
            v.memset(minus_one[:], -1.0).then_inc(f_out, 1)
            v.memset(carry[:], 0.0).then_inc(stored, 16)
            v.memset(v_sb[:, :, :, DV:VW], 1.0).then_inc(const_set, 1)
            def low_part(g):
                dve.wait_ge(hi_split, g + 1)
                cols = slice(WSTART[g], WEND[g])
                v.tensor_tensor(w_lo[:, :, cols], stage_w[:, :, cols], w_hi[:, :, cols].bitcast(f32), ALU.subtract).then_inc(w_split[g], 1)

            for n, name in enumerate(("XT0", "XT1", "XTE")):
                step(name, 0, n, first_banks[n])
            low_part(0)
            dve.wait_ge(rope_loaded, 16)
            for n, what in enumerate(PJOBS):
                rotate(n, what)
                if what == "E":
                    low_part(1)

            def body(it, kind):
                state["kind"] = kind
                st = state_of(it, kind)
                for q in range(Q_N):
                    g, j = q // 4, q % 4
                    quad = it * Q_N + q
                    for pair, place in ((0, "A"), (1, "B")):
                        row_max(it * S_N + q * 2 + pair, pair, (q * 2 + pair) % 4)
                        if pair == 0 and (kind != "first" or q >= 2):
                            normalize(quad - 2, q % 2)
                            if q in (2, 4) and kind != "first":
                                dve.wait_ge(misc_done, st["base"] + 1 + q // 2)
                            normalize_out(quad - 2, q % 2, (q - 2) % Q_N // 4, (q - 2) % 4)
                        for name, arg, idx in walk(kind, it, (q, place), st):
                            step(name, arg, idx)
                        p = proj_at(g, j, place)
                        if p and not (kind == "last" and g == 3):
                            if p[0] == 18:
                                dve.wait_ge(rope_loaded, it * 16 + 32)
                            rotate(P_FIRST + it * P_N + p[0], p[1])
                    for name, arg, idx in walk(kind, it, (q, "C"), st):
                        step(name, arg, idx)

            chunks(dve, body)
            state["kind"] = "tail"
            for n in (2, 1):
                normalize(NCH * Q_N - n, n % 2)
                normalize_out(NCH * Q_N - n, n % 2, 3, 4 - n)
            for name, arg, idx in tail_steps():
                step(name, arg, idx)

        @block.scalar
        def _(act):
            sc = nc.scalar

            def exps(quad, q, pair):
                idx = 2 * quad + pair
                act.wait_ge(max_done, idx + 1)
                if not (isinstance(quad, int) and quad < 2):
                    act.wait_ge(t_done, quad - 1)
                for u in range(2):
                    last = sc.activation(prob[:, q % 2, 2 * pair + u, :], s_ps[pair][:, u * KEYS:(u + 1) * KEYS], ACT.Exp,
                                         bias=neg_max[:, (q * 2 + pair) % 4, u:u + 1], scale=1.0)
                last.then_inc(exp_done, 1)

            def gather_front(quad, q):
                act.wait_ge(exp_done, 2 * quad + 2)
                sc.copy(prob_f[:, q % 2, :, :], prob[:, q % 2, :, 0:FRONT]).then_inc(front_ready, 1)

            def copy_transposed(quad, par):
                act.wait_ge(t_done, quad + 1)
                if not (isinstance(quad, int) and quad < 2):
                    act.wait_ge(pv_done, quad - 1)
                sc.copy(prob_t[:, par, 0:4 * P], pt_ps[:, :])
                sc.copy(prob_t[:, par, 4 * P:], pf_ps[:, 0:P]).then_inc(pt_ready, 1)

            def spread_keys(stage, par):
                act.wait_ge(rope_add, stage * P_FIRST + 2)
                sc.copy(k_sb[:, par, 0, FRONT:FRONT + BLK], k_ext[:, 0:BLK])
                sc.copy(k_sb[:, par, 1:, FRONT:FRONT + BLK], k_sb[:, par, 0:NBLK - 1, FRONT + BLK:])
                sc.copy(k_sb[:, par, :, 0:FRONT], k_ext[:, None, BLK:].broadcast_to([P, NBLK, FRONT])).then_inc(k_ready, 1)

            def apply_norm(dst, src, a, work, done):
                for t in (2 * a, 2 * a + 1):
                    last = sc.activation(dst[:, t, :], src[:, t, :], ACT.Identity, bias=work[:, 2, t:t + 1], scale=work[:, 1, t:t + 1])
                last.then_inc(done, 1)

            def free_x1(arg, kind):
                if kind in ("store", "thought"):
                    act.wait_ge(x1_stored, arg * 16)
                else:
                    act.wait_ge(x1_stored, NSTORE * 16)
                    act.wait_ge(f_added, (arg - NSTORE) * 4 + 1)

            def step(name, arg, idx, kind, misc=misc):
                if name in ("OT0", "OT1", "X1T0", "X1T1", "XT0", "XT1", "XTE"):
                    act.wait_ge(misc_done, idx + 1)
                if name in ("XT0", "XT1", "XTE"):
                    if name == "XT0" and not (isinstance(arg, int) and arg == 0):
                        act.wait_ge(proj_done, arg * P_N)
                    if name == "XTE":
                        sc.copy(x_hi[:, :, 0:EXT], misc[:, 0:KT * EXT].rearrange("p (k n) -> p k n", k=KT)).then_inc(xhi_ready, 1)
                    else:
                        sc.copy(x_hi[:, int(name[2]), EXT:], misc[:, :]).then_inc(xhi_ready, 1)
                elif name in ("OT0", "OT1"):
                    a = int(name[2])
                    dst = e_t[:, :, a * 4 * BLK:(a + 1) * 4 * BLK].rearrange("p h (u q) -> p h u q", u=4)
                    sc.copy(dst, misc[:, :].rearrange("p (u h q) -> p h u q", u=4, h=2)).then_inc(misc_read, 1)
                elif name in ("X1T0", "X1T1"):
                    a = int(name[3])
                    sc.copy(e_t[:, :, a * 2 * P:(a + 1) * 2 * P], misc[:, :].rearrange("p (k n) -> p k n", k=KT)).then_inc(misc_read, 1)
                elif name in ("NM0", "NM1"):
                    a = int(name[2])
                    act.wait_ge(rstd_ready, arg * 2 + a + 1)
                    if a == 0 and not (isinstance(arg, int) and arg == 0):
                        free_x1(arg, kind)
                    apply_norm(x1, y, a, rstd, x1_ready)
                elif name in ("G0", "G1"):
                    act.wait_ge(misc_read, idx + 1)
                    a = int(name[1])
                    src = z[:, 2 * a:2 * a + 2, :].rearrange("p t d -> p (t d)")
                    dst = src
                    if kind in ("store", "thought"):
                        dst = store[:, 1, bass.ds(arg, 1), a * 2 * D:(a + 1) * 2 * D].rearrange("p a d -> p (a d)")
                    sc.activation(dst, src, ACT.Tanh, scale=0.5).then_inc(tanh_ready, 1)
                elif name == "TH":
                    act.wait_ge(misc_read, idx + 1)
                    sc.activation(hid_g[:], hid[:], ACT.Gelu).then_inc(gelu_ready, 1)
                elif name in ("FC0", "FC1"):
                    a = int(name[2])
                    act.wait_ge(f_rstd, 4 * arg[2] + a + 1)
                    act.wait_ge(f_out, 2 * arg[2] + 1)
                    apply_norm(f2, f1, a, frstd[0], f_norm)
                elif name in ("FE0", "FE1"):
                    a = int(name[2])
                    fi = arg[2]
                    act.wait_ge(f_rstd, 4 * fi + a + 3)
                    if a == 0:
                        act.wait_ge(stored, fi * 32 + 16)
                    apply_norm(f_o, f2, a, frstd[1], f_out)

            def high_part(g):
                act.wait_ge(w_loaded[g], 16)
                cols = slice(WSTART[g], WEND[g])
                sc.copy(w_hi[:, :, cols], stage_w[:, :, cols]).then_inc(hi_split, 1)

            for n, name in enumerate(("XT0", "XT1", "XTE")):
                step(name, 0, n, "first", first_banks[n])
            for g in range(GROUPS):
                high_part(g)
            spread_keys(0, 0)

            def body(it, kind):
                st = state_of(it, kind)
                for q in range(Q_N):
                    g, j = q // 4, q % 4
                    quad = it * Q_N + q
                    for pair, place in ((0, "A"), (1, "B")):
                        copies = [s for s in walk(kind, it, (q, place), st)]
                        early = [s for s in copies if pair == 1 and s[0] in PE_FED]
                        for name, arg, idx in early:
                            step(name, arg, idx, kind)
                        exps(quad, q, pair)
                        if pair == 1:
                            gather_front(quad, q)
                        for name, arg, idx in copies:
                            if (name, arg, idx) not in early:
                                step(name, arg, idx, kind)
                        if pair == 0 and not (kind == "first" and q == 0):
                            copy_transposed(quad - 1, (q - 1) % 2)
                        if place == "A" and j > 0:
                            p = proj_at(g, j - 1, "B")
                            if p and p[1] == "E" and not (kind == "last" and g == 3):
                                spread_keys(it * GROUPS + g + 1, (g + 1) % 2)
                    for name, arg, idx in walk(kind, it, (q, "C"), st):
                        step(name, arg, idx, kind)

            chunks(act, body)
            copy_transposed(NCH * Q_N - 1, 1)
            for name, arg, idx in tail_steps():
                step(name, arg, idx, "tail")

        @block.gpsimd
        def _(pool):
            gp = nc.gpsimd

            def add(stage, par, what):
                k = PJOBS.index(what)
                pool.wait_ge(rope_mul, stage * P_FIRST + k + 1)
                lo, hi = columns(what)
                c, s = rope_c[:, k % 2, 0:hi - lo], rope_s[:, k % 2, 0:hi - lo]
                if what == "K":
                    if not (isinstance(stage, int) and stage < 2):
                        pool.wait_ge(s_done, (stage - 1) * 8)
                    if not (isinstance(stage, int) and stage == 0):
                        pool.wait_ge(k_ready, stage)
                    gp.tensor_tensor(k_ext[:, :], c[:, 0:EXT], s[:, 0:EXT], ALU.add)
                    c, s = c[:, EXT:], s[:, EXT:]
                    dst = k_sb[:, par, 0:3, FRONT + BLK:]
                elif what == "E":
                    dst = k_sb[:, par, 3:, FRONT + BLK:]
                else:
                    dst = q_sb[:, par, what // 2, :, what % 2 * BLK:(what % 2 + 1) * BLK]
                c, s = (a.rearrange("p (u n) -> p u n", n=BLK) for a in (c, s))
                gp.tensor_tensor(dst, c, s, ALU.add).then_inc(rope_add, 1)

            def inverse_root(m, a, work, eps, ve, n, done):
                h = slice(2 * a, 2 * a + 2)
                gp.tensor_tensor(work[:, 0, h], m[:, h, 1], eps[:, h], ALU.add).then_inc(ve, 1)
                gp.tensor_tensor(work[:, 2, h], m[:, h, 0], minus_one[:, h], ALU.mult).then_inc(ve, 1)
                pool.wait_ge(ve, 3 * n + 2)
                gp.tensor_tensor(work[:, 1, h], work[:, 0, h], half_pow[:, h], ALU.pow).then_inc(ve, 1)
                pool.wait_ge(ve, 3 * n + 3)
                gp.tensor_tensor(work[:, 2, h], work[:, 2, h], work[:, 1, h], ALU.mult).then_inc(done, 1)

            def th_inverse_root(n):
                pool.wait_ge(th_mv, n + 1)
                gp.tensor_tensor(trs[:, 0:1], tmv[:, 1:2], eps2[0:BATCH, 0:1], ALU.add).then_inc(th_ve, 1)
                pool.wait_ge(th_ve, n + 1)
                gp.tensor_tensor(trs[:, 1:2], trs[:, 0:1], half_pow[0:BATCH, 0:1], ALU.pow).then_inc(th_rstd, 1)

            def step(name, arg, idx):
                if name in ("BN0", "BN1"):
                    a = int(name[2])
                    pool.wait_ge(mv_ready, arg * 2 + a + 1)
                    inverse_root(mv, a, rstd, eps1, ve_ready, arg * 2 + a, rstd_ready)
                elif name in ("TX", "TA") or name == "TD" and arg < STEPS - 1:
                    th_inverse_root({"TX": 0, "TA": 1}.get(name, 2 + arg))
                elif name[0] == "F":
                    src, n, fi = arg
                    xs, _, _ = sources(src, n)
                    a = int(name[2])
                    tiles = slice(2 * a, 2 * a + 2)
                    if name[1] == "A":
                        pool.wait_ge(f_gated, 2 * fi + a + 2)
                        if src == "S":
                            pool.wait_ge(x1_stored, n * 16 + 16)
                        gp.tensor_tensor(f1[:, tiles, :], f1[:, tiles, :], xs[:, tiles, :], ALU.add).then_inc(f_sum, 1)
                    elif name[1] == "X":
                        if src == "E":
                            pool.wait_ge(x1_ready, n * 2 + a + 1)
                        gp.tensor_tensor(f_x[:, tiles, :], xs[:, tiles, :], out_beta[:, None, :].broadcast_to([P, 2, D]), ALU.add).then_inc(f_beta, 1)
                    elif name[1] in "BD":
                        first = name[1] == "B"
                        k = 4 * fi + a + (0 if first else 2)
                        pool.wait_ge(f_mv, k + 1)
                        inverse_root(fmv, a, frstd[0 if first else 1], eps2 if first else eps1, f_ve, k, f_rstd)
                    elif name[1] == "G":
                        pool.wait_ge(f_beta, 2 * fi + a + 1)
                        pool.wait_ge(f_scaled, 2 * fi + a + 1)
                        gp.tensor_tensor(f2[:, tiles, :], f2[:, tiles, :], f_x[:, tiles, :], ALU.add).then_inc(f_added, 1)

            pool.wait_ge(const_set, 1)
            for what in PJOBS:
                add(0, 0, what)
            for g in range(2, GROUPS):
                pool.wait_ge(hi_split, g + 1)
                cols = slice(WSTART[g], WEND[g])
                gp.tensor_tensor(w_lo[:, :, cols], stage_w[:, :, cols], w_hi[:, :, cols].bitcast(f32), ALU.subtract).then_inc(w_split[g], 1)

            def body(it, kind):
                st = state_of(it, kind)
                for q in range(Q_N):
                    g, j = q // 4, q % 4
                    for place in "ABC":
                        for name, arg, idx in walk(kind, it, (q, place), st):
                            step(name, arg, idx)
                        p = proj_at(g, j, place)
                        if p and not (kind == "last" and g == 3):
                            add(it * GROUPS + g + 1, (g + 1) % 2, p[1])

            chunks(pool, body)
            for name, arg, idx in tail_steps():
                step(name, arg, idx)


def kernel(**inputs):
    import numpy as np
    import concourse.bacc as bacc
    from concourse.bass_utils import run_bass_kernel_spmd

    a = {k: np.asarray(v) for k, v in inputs.items()}
    import ml_dtypes
    bf = ml_dtypes.bfloat16
    f = np.float32

    def split_rows(w, tiles):
        return np.ascontiguousarray(w.reshape(tiles, P, -1).transpose(1, 0, 2))

    x = a["L0_attn_x"]
    steps = []
    for it in range(NCH):
        b, c = it % BATCH, 1 - it // BATCH
        prev = max(c * CHUNK - BLK, 0)
        steps.append(np.concatenate([x[b, prev:prev + BLK], x[b, :FRONT], x[b, c * CHUNK:(c + 1) * CHUNK]]))
    order = np.concatenate([np.arange(0, P, 2), np.arange(1, P, 2)])
    wq = a["L0_attn_wq"].reshape(D, HEADS, P)[:, :, order].reshape(D, HEADS * P)
    wk = a["L0_attn_wk"].reshape(D, GROUPS, P)[:, :, order].reshape(D, GROUPS * P)
    parts = []
    for g in range(GROUPS):
        parts += [wk[:, g * P:(g + 1) * P], wq[:, g * REP * P:(g + 1) * REP * P]]
        if g == 0:
            parts.append(a["L0_attn_wv"])
    w_all = split_rows(np.concatenate(parts, axis=1), KT)
    wo_t = np.ascontiguousarray(a["L0_attn_wo"].reshape(HEADS // 2, 2, DV, D).transpose(0, 2, 1, 3).reshape(P, 2, D))
    inv = (1.0 / 10000.0 ** (np.arange(0, P, 2)[:P // 2].astype(f) / P))
    ang = np.outer(np.arange(SEQ, dtype=f), inv.astype(f))
    cos, sin = np.cos(ang).T.astype(np.float64), np.sin(ang).T.astype(np.float64)
    scale = float(P) ** -0.25
    rope = np.empty((2, P, 2, XW), f)
    for half in range(2):
        c = 1 - half
        prev = max(c * CHUNK - BLK, 0)
        pos = np.concatenate([np.arange(prev, prev + BLK), np.arange(FRONT), np.arange(c * CHUNK, (c + 1) * CHUNK)])
        rope[half, :, 0] = np.concatenate([cos[:, pos], cos[:, pos]]) * scale
        rope[half, :, 1] = np.concatenate([sin[:, pos], -sin[:, pos]]) * scale
    NEG = -1e30
    i, k = np.arange(BLK)[:, None], np.arange(2 * BLK)[None, :]
    std = np.where((k > i) & (k <= i + BLK), 0.0, NEG)
    edge = np.zeros((2, BLK, 2, KEYS))
    edge[:, :, :, FRONT:] = std[:, None, :]
    edge[1, :, 0, :FRONT + BLK] = NEG
    edge[1, :, 1, :FRONT] = np.where(np.arange(FRONT)[None, :] <= i, 0.0, NEG)
    std2, edge2 = np.concatenate([std, std]).astype(bf), np.concatenate([edge, edge], axis=1).astype(bf)
    vec = lambda names, n: np.ascontiguousarray(np.broadcast_to(np.stack([a["L0_ffn_" + x] for x in names]), (n, len(names), D)))
    arrays = {
        "x_steps": np.stack(steps), "w_all": w_all, "wo_t": wo_t, "gate_t": split_rows(a["L0_ffn_gate_w"], KT),
        "agg_t": split_rows(a["L0_ffn_agg_w"], KT), "bc_t": split_rows(a["L0_ffn_bc_w"], KT),
        "d1_t": split_rows(a["L0_ffn_d1_w"], KT), "d2_t": split_rows(a["L0_ffn_d2_w"], HT),
        "d1b_t": np.ascontiguousarray(a["L0_ffn_d1_b"].reshape(HT, P).T),
        "vec128": vec(["gate_b", "out_gamma", "out_beta", "bc_b"], P),
        "vec4": vec(["in_gamma", "in_beta", "agg_b", "pn_gamma", "pn_beta", "d2_b"], BATCH),
        "rope": rope, "mask_std": std2, "mask_edge": edge2, "ident_bf": np.eye(P).astype(bf), "ident_f": np.eye(P, dtype=f),
    }
    nc = bacc.Bacc("TRN2", target_bir_lowering=False, num_devices=1)
    args = [nc.dram_tensor(n, v.shape, mybir.dt.from_np(v.dtype), kind="ExternalInput").ap() for n, v in arrays.items()]
    out = nc.dram_tensor("out", (NCH, CHUNK, D), mybir.dt.float32, kind="ExternalOutput").ap()
    build(nc, *args, out)
    r = run_bass_kernel_spmd(nc, [arrays], core_ids=[0])
    got = r.results[0]["out"]
    return np.ascontiguousarray(got.reshape(2, BATCH, CHUNK, D)[::-1].transpose(1, 0, 2, 3).reshape(BATCH, SEQ, D))
```

```python
from contextlib import ExitStack

import concourse.bass as bass
from concourse import mybir
from concourse.alu_op_type import AluOpType as ALU

P = 128
D = 256
KT = D // P
SEQ, BATCH = 1024, 4
CHUNK = 512
NCH = SEQ * BATCH // CHUNK
NSTORE = BATCH
TILES = CHUNK // P
HEADS, GROUPS, REP = 16, 4, 4
DV = D // HEADS
VW = DV + 1
BLK, FRONT = 64, 32
NBLK = CHUNK // BLK
EXT = BLK + FRONT
KSPLIT = EXT + 3 * BLK
XW = EXT + CHUNK
KEYS = FRONT + 2 * BLK
H = 1024
HT = H // P
STEPS = 4
WPART, WV0, WV = (1 + REP) * P, (1 + REP) * P, GROUPS * DV
WALL = GROUPS * WPART + WV
WSTART = [0] + [WV + g * WPART for g in range(1, GROUPS)]
WEND = [WV + (g + 1) * WPART if g else WPART for g in range(GROUPS)]
EPS1, EPS2 = 1e-5, 1e-6

EPILOGUE = {(2, "A"): ["OT0"], (2, "B"): ["OP0"], (2, "C"): ["BN0"], (3, "A"): ["OT1"], (3, "B"): ["OP1"], (3, "C"): ["BN1"],
            (4, "A"): ["NM0"], (4, "B"): ["X1T0", "NM1"], (5, "A"): ["G0"], (5, "B"): ["X1T1"], (6, "A"): ["G1"]}
EPILOGUE_THOUGHT = EPILOGUE | {(3, "B"): ["OP1", "NM0"], (4, "A"): ["X1T0"], (4, "B"): ["G0", "NM1"], (5, "A"): ["X1T1"],
                               (5, "B"): ["G1"], (6, "A"): []}
PREPARE = {(11, "B"): ["XT0"], (12, "A"): ["XT1"], (12, "B"): ["XTE"]}
THOUGHT = [("TX", 0, (5, "B")), ("TM", 0, (5, "C")), ("TN", 0, (6, "A")), ("TA", 0, (6, "B")), ("TM", 1, (6, "C"))]
for n in range(STEPS):
    THOUGHT += [("TT", n, (7 + 2 * n, "A")), ("TH", n, (7 + 2 * n, "B")), ("TD", n, (8 + 2 * n, "A"))]
    THOUGHT += [("TM", n + 2, (8 + 2 * n, "C"))] if n < STEPS - 1 else []
THOUGHT += [("TU", 0, (14, "B")), ("TB0", 0, (15, "A")), ("TB1", 0, (15, "B"))]
PE_FED = ("V0", "V1", "OT0", "OT1", "X1T0", "X1T1", "XT0", "XT1", "XTE")
FINAL = ["FA0", "FA1", "FX0", "FB0", "FB1", "FX1", "FC0", "FC1", "FG0", "FG1", None, "FD0", "FD1", None, None, "FE0", "FE1"]
FINAL_SPREAD = FINAL[:8] + [None] * 7 + ["FG0", "FG1", None, "FD0", "FD1", None, None, "FE0", "FE1"]
FINAL_S, FINAL_E, FINAL_S3 = 0, 8, 13
MISC_JOBS = {"V0", "V1", "OT0", "OT1", "OP0", "OP1", "X1T0", "X1T1", "G0", "G1", "XT0", "XT1", "XTE", "TN", "TA", "TT", "TH", "TD", "TU", "TB0", "TB1"}
N_EPI, N_PREP, N_THOUGHT = 8, 3, sum(name in MISC_JOBS for name, _, _ in THOUGHT)
PROJECT = {(0, "A"): "K", (0, "B"): "E", (1, "A"): 0, (1, "B"): 1, (2, "A"): 2, (3, "A"): 3}
PROJECT_LAST = {(1, "A"): "K", (1, "B"): "E", (2, "A"): 0, (2, "B"): 1, (3, "A"): 2, (3, "B"): 3}
PJOBS = ["K", "E", 0, 1, 2, 3]


def plan(it, kind):
    steps = {(1, "A"): [("V0", it)], (1, "B"): [("V1", it)]}
    if kind == "first":
        steps[4, "C"], steps[5, "C"] = [("WH", 0)], [("WL", 0)]

    def add(at, names, arg):
        steps.setdefault(at, []).extend((n, arg) for n in names)

    if kind != "first":
        for at, names in (EPILOGUE_THOUGHT if kind == "thought" else EPILOGUE).items():
            add(at, names, it - 1)
    if kind == "thought":
        for name, n, at in THOUGHT:
            add(at, [name], n)
    if kind != "last":
        for at, names in PREPARE.items():
            add(at, names, it + 1)
    if kind in ("final", "last"):
        starts = [(FINAL_S, ("S", it - 5, (it - 5) * 2)), (FINAL_E, ("E", it - 1, (it - 5) * 2 + 1))]
        if kind == "last":
            starts.append((FINAL_S3, ("S", 3, 6)))
        for slot, arg in starts:
            for n, name in enumerate(FINAL_SPREAD if slot == FINAL_S else FINAL):
                at = (slot + n // 3, "ABC"[n % 3])
                if name and at[0] < 16:
                    add(at, [name], arg)
    if kind == "last":
        add((15, "B"), ["OT0"], it)
        add((15, "C"), ["OP0", "BN0"], it)
    return steps


def misc_base(it):
    if isinstance(it, int) and it == 0:
        return N_PREP
    return it * (2 + N_EPI + N_PREP) - N_EPI + N_PREP


def build(nc, x_steps, w_all, wo_t, gate_t, agg_t, bc_t, d1_t, d2_t, d1b_t, vec128, vec4, rope, mask_std,
          mask_edge, ident_bf, ident_f, out):
    f32, f32r, bf16 = mybir.dt.float32, mybir.dt.float32r, mybir.dt.bfloat16
    ACT = mybir.ActivationFunctionType
    AX = mybir.AxisListType
    ctx = ExitStack()
    with ctx:
        sb = lambda n, s, d=f32: ctx.enter_context(nc.sbuf_tensor(n, s, d))
        ps = lambda n, s: ctx.enter_context(nc.psum_tensor(n, s, f32))
        sem = lambda n: ctx.enter_context(nc.semaphore(n))

        w_hi, w_lo = sb("w_hi", [P, KT, WALL], f32r), sb("w_lo", [P, KT, WALL], f32r)
        og_hi, og_lo = sb("og_hi", [P, 2, KT, D], f32r), sb("og_lo", [P, 2, KT, D], f32r)
        agg_w, bc_w = sb("agg_w", [P, KT, D]), sb("bc_w", [P, KT, D])
        d1_w, d2_w, d1_b = sb("d1_w", [P, KT, H]), sb("d2_w", [P, HT, D]), sb("d1_b", [P, HT])
        v128, v4 = sb("v128", [P, 4, D]), sb("v4", [BATCH, 6, D])
        gate_b, out_gamma, out_beta, bc_b = (v128[:, n, :] for n in range(4))
        in_gamma, in_beta, agg_b, pn_gamma, pn_beta, d2_b = (v4[:, n, :] for n in range(6))
        rope_sb = sb("rope_sb", [P, 2, XW])
        std_sb, edge_sb = sb("std_sb", [P, 2 * BLK], bf16), sb("edge_sb", [P, 2, KEYS], bf16)
        id_bf, id_f = sb("id_bf", [P, P], bf16), sb("id_f", [P, P])
        x_in = sb("x_in", [P, 1 + TILES, D])
        wv_sb = sb("wv_sb", [P, KT, 2 * WV], f32r)
        v_low = sb("v_low", [P, 3, GROUPS, DV])
        x_hi, x_lo = sb("x_hi", [P, KT, XW], f32r), sb("x_lo", [P, KT, XW], f32r)
        rope_c, rope_s = sb("rope_c", [P, 2, CHUNK]), sb("rope_s", [P, 2, CHUNK])
        q_sb = sb("q_sb", [P, 2, 2, NBLK, P])
        k_ext, k_sb = sb("k_ext", [P, EXT]), sb("k_sb", [P, 2, NBLK, KEYS])
        v_sb, vf_sb = sb("v_sb", [P, NBLK, GROUPS, VW]), sb("vf_sb", [P, GROUPS, 4 * VW])
        neg_max = sb("neg_max", [P, 4, 2])
        prob = sb("prob", [P, 2, 4, KEYS])
        prob_f = sb("prob_f", [P, 2, 4, FRONT])
        prob_t = sb("prob_t", [P, 2, 5 * P])
        rcp, o_sb = sb("rcp", [P, 2, 4]), sb("o_sb", [P, NBLK, P])
        e_hi, e_lo = (sb(n, [P, KT, 2 * P], f32r) for n in ("e_hi", "e_lo"))
        y, x1, z = sb("y", [P, TILES, D]), sb("x1", [P, TILES, D]), sb("z", [P, TILES, D])
        og_w = x1[:, :, :].rearrange("p (a k) d -> p a k d", a=2)
        store = sb("store", [P, 2, NSTORE, TILES * D])
        stats, mv = sb("stats", [P, TILES, 6]), sb("mv", [P, TILES, 2])
        rstd, half_pow = sb("rstd", [P, 3, TILES]), sb("half_pow", [P, TILES])
        minus_one = sb("minus_one", [P, TILES])
        eps1, eps2 = sb("eps1", [P, TILES]), sb("eps2", [P, TILES])
        carry = sb("carry", [1, 1])
        f1 = d1_w[:, 0, :].rearrange("p (t d) -> p t d", t=TILES)
        f2 = d1_w[:, 1, :].rearrange("p (t d) -> p t d", t=TILES)
        f_x, f_o = d2_w[:, 0:TILES, :], d2_w[:, TILES:2 * TILES, :]
        fstats, fmv = sb("fstats", [P, TILES, 6]), sb("fmv", [P, TILES, 2])
        frstd = [sb(f"frstd{n}", [P, 3, TILES]) for n in range(2)]
        bc_sb = sb("bc_sb", [P, BATCH, D])
        last_x, th, tn = (bc_sb[0:BATCH, n, :] for n in range(3))
        tst, tmv, trs = sb("tst", [BATCH, 6]), sb("tmv", [BATCH, 2]), sb("trs", [BATCH, 2])
        t_t, hid, hid_g = sb("t_t", [P, KT, BATCH]), sb("hid", [P, HT, BATCH]), sb("hid_g", [P, HT, BATCH])
        stage_w = store[:, :, :, :].rearrange("p a n d -> p (a n d)")[:, 0:KT * WALL].rearrange("p (k n) -> p k n", k=KT)

        pj = [ps(f"pj{n}", [P, 512]) for n in range(2)]
        s_ps = [ps(f"s_ps{n}", [P, 512]) for n in range(2)]
        pt_ps, pf_ps = ps("pt_ps", [P, 512]), ps("pf_ps", [P, 512])
        pv_ps, misc = ps("pv_ps", [P, 512]), ps("misc", [P, 512])
        misc_bank, first_banks = misc, [misc, s_ps[0], s_ps[1]]
        v_ps = misc[:, 0:3 * 2 * WV].rearrange("p (t s g d) -> p t s g d", t=3, s=2, g=GROUPS)

        w_loaded, id_loaded, c_loaded, ffn_loaded = [sem(f"w_loaded{g}") for g in range(GROUPS)], sem("id_loaded"), sem("c_loaded"), sem("ffn_loaded")
        x_loaded, rope_loaded, edge_loaded, res_loaded = sem("x_loaded"), sem("rope_loaded"), sem("edge_loaded"), sem("res_loaded")
        const_step, const_set, hi_split, w_split = sem("const_step"), sem("const_set"), sem("hi_split"), [sem(f"w_split{g}") for g in range(GROUPS)]
        proj_done, rope_mul, rope_add, k_ready = sem("proj_done"), sem("rope_mul"), sem("rope_add"), sem("k_ready")
        s_done, max_done, exp_done = sem("s_done"), sem("max_done"), sem("exp_done")
        t_done, pt_ready, pv_done, rcp_done, o_ready, front_ready = sem("t_done"), sem("pt_ready"), sem("pv_done"), sem("rcp_done"), sem("o_ready"), sem("front_ready")
        misc_done, misc_read, xhi_ready = sem("misc_done"), sem("misc_read"), sem("xhi_ready")
        bn_done, mv_ready, ve_ready, rstd_ready, x1_ready = sem("bn_done"), sem("mv_ready"), sem("ve_ready"), sem("rstd_ready"), sem("x1_ready")
        tanh_ready, x1_stored, tail_x = sem("tanh_ready"), sem("x1_stored"), sem("tail_x")
        f_gated, f_sum, f_bn, f_mv, f_ve, f_rstd = sem("f_gated"), sem("f_sum"), sem("f_bn"), sem("f_mv"), sem("f_ve"), sem("f_rstd")
        f_norm, f_scaled, f_added, stored = sem("f_norm"), sem("f_scaled"), sem("f_added"), sem("stored")
        f_beta, f_out, v_low_ready = sem("f_beta"), sem("f_out"), sem("v_low_ready")
        og_split, og_ready, ehi_ready = sem("og_split"), sem("og_ready"), sem("ehi_ready")
        th_rows, th_mv, th_ve, th_rstd = sem("th_rows"), sem("th_mv"), sem("th_ve"), sem("th_rstd")
        th_link, gelu_ready = sem("th_link"), sem("gelu_ready")

        S_N, Q_N, P_N = 32, 16, 24
        P_FIRST = len(PJOBS)

        def thought_jobs(kind):
            return N_THOUGHT if kind in ("final", "last", "tail") else 0

        def walk(kind, it, place, state):
            for name, arg in state["steps"].get(place, []):
                idx = state["base"] + state["n"]
                if name in MISC_JOBS:
                    state["n"] += 1
                yield name, arg, idx

        def state_of(it, kind):
            return {"steps": plan(it, kind), "base": misc_base(it) + thought_jobs(kind), "n": 0}

        def columns(what):
            return {"K": (0, KSPLIT), "E": (KSPLIT, XW)}.get(what, (EXT, XW))

        def proj_at(g, j, place):
            table = PROJECT_LAST if g == 3 else PROJECT
            what = table.get((j, place))
            return None if what is None else (6 * g + PJOBS.index(what), what)

        def chunks(eng, body):
            body(0, "first")
            with eng.Fori(1, 4) as it:
                body(it, "store")
            body(4, "thought")
            with eng.Fori(5, 7) as it:
                body(it, "final")
            body(7, "last")

        s3, e7 = ("S", 3, 6), ("E", 7, 7)
        tail_plan = [("FG1", s3), ("FD0", s3), ("OT1", 7), ("NM0", 7), ("FX0", e7), ("FD1", s3), ("OP1", 7), ("FE0", s3), ("BN1", 7), ("X1T0", 7), ("NM1", 7), ("G0", 7), ("FE1", s3),
                     ("FX1", e7), ("X1T1", 7), ("FA0", e7), ("FB0", e7), ("G1", 7), ("FC0", e7), ("FA1", e7), ("FB1", e7)]
        tail_plan += [(n, e7) for n in ("FG0", "FD0", "FC1", "FG1", "FD1", "FE0", "FE1")]

        def tail_bank(name):
            return {"X1T0": s_ps[0], "X1T1": s_ps[1]}.get(name, misc)

        def tail_steps():
            idx = misc_base(7) + N_THOUGHT + 2 + N_EPI + 2
            for name, arg in tail_plan:
                yield name, arg, idx
                if name in MISC_JOBS:
                    idx += 1

        thought_over = misc_base(5) + N_THOUGHT

        def sources(src, n):
            if src == "S":
                at = bass.ds(n, 1)
                xs, ts = (store[:, k, at, :].rearrange("p a (t d) -> p (a t) d", t=TILES) for k in range(2))
                return xs, ts, bc_sb[:, at, :]
            return x1[:, :, :], z[:, :, :], bc_sb[:, bass.ds(n - NSTORE, 1), :]

        block = ctx.enter_context(nc.Block())

        @block.sync
        def _(sp):
            def load_x(n):
                sp.dma_start(x_in[0:EXT, 0, :], x_steps[bass.ds(n, 1), 0:EXT, :].rearrange("a p d -> (a p) d")).then_inc(x_loaded, 16)
                sp.dma_start(x_in[:, 1:, :], x_steps[bass.ds(n, 1), EXT:XW, :].rearrange("a (t p) d -> (a p) t d", p=P)).then_inc(x_loaded, 16)

            def load_rope(n, half):
                sp.dma_start(rope_sb[:], rope[bass.ds(half, 1)].rearrange("a p c n -> (a p) c n")).then_inc(rope_loaded, 16)

            def load_edge(half):
                sp.dma_start(edge_sb[:], mask_edge[bass.ds(half, 1)].rearrange("a p u n -> (a p) u n")).then_inc(edge_loaded, 16)

            def load_w(g):
                cols = slice(WSTART[g], WEND[g] if g else WPART + WV)
                sp.dma_start(stage_w[:, :, cols], w_all[:, :, cols]).then_inc(w_loaded[g], 16)

            sp.dma_start(id_f[:], ident_f).then_inc(id_loaded, 16)
            load_x(0)
            load_w(0)
            load_rope(0, 0)
            sp.dma_start(id_bf[:], ident_bf).then_inc(c_loaded, 16)
            sp.dma_start(std_sb[:], mask_std).then_inc(c_loaded, 16)
            load_edge(0)
            for g in range(1, GROUPS):
                load_w(g)
            for dst, src in ((og_w[:, 0, :, :], wo_t), (og_w[:, 1, :, :], gate_t), (agg_w[:], agg_t), (bc_w[:], bc_t), (d1_w[:], d1_t),
                             (d2_w[:], d2_t), (d1_b[:], d1b_t), (v128[:], vec128), (v4[:], vec4)):
                sp.dma_start(dst, src).then_inc(ffn_loaded, 16)

            def store_x1(n):
                sp.dma_start(store[:, 0, bass.ds(n, 1), :].rearrange("p a d -> p (a d)"), x1[:, :, :].rearrange("p t d -> p (t d)")).then_inc(x1_stored, 16)

            def output(n, fi):
                for a in range(2):
                    sp.wait_ge(f_out, 2 * fi + a + 2)
                    sp.dma_start(out[bass.ds(n, 1), a * 2 * P:(a + 1) * 2 * P].rearrange("a (t p) d -> (a p) t d", p=P),
                                 f_o[:, 2 * a:2 * a + 2, :]).then_inc(stored, 16)

            def body(it, kind):
                if kind != "last":
                    sp.wait_ge(misc_done, misc_base(it) + thought_jobs(kind))
                    load_x(it + 1)
                if kind != "first":
                    sp.wait_ge(x1_ready, it * 2)
                if kind in ("store", "thought"):
                    store_x1(it - 1)
                if kind == "thought":
                    sp.wait_ge(x1_stored, (BATCH - 1) * 16)
                    sp.dma_start(last_x[0:BATCH - 1], store[P - 1:P, 0, 0:BATCH - 1, (TILES - 1) * D:]).then_inc(tail_x, 16)
                    sp.dma_start(last_x[BATCH - 1:], x1[P - 1:P, TILES - 1, :]).then_inc(tail_x, 16)
                sp.dma_start(y[:], x_steps[bass.ds(it, 1), EXT:XW, :].rearrange("a (t p) d -> (a p) t d", p=P)).then_inc(res_loaded, 16)
                if kind in ("final", "last"):
                    output(it - 5, (it - 5) * 2)
                if kind != "last":
                    half = {"first": 0, "thought": 1, "final": 1}.get(kind)
                    nxt = half if half is not None else (it + 1) // NSTORE
                    sp.wait_ge(rope_mul, it * P_N + P_N)
                    load_rope(it + 1, nxt)
                if kind in ("final", "last"):
                    output(it - 1, (it - 5) * 2 + 1)
                if kind != "last":
                    sp.wait_ge(s_done, it * S_N + 3 * 8 + 2)
                    load_edge(nxt)

            chunks(sp, body)
            output(3, 6)
            output(7, 7)
            sp.wait_ge(stored, NCH * 32 + 16)

        @block.tensor
        def _(pe):
            mm = nc.tensor.matmul

            def split_mm(o, w, x):
                for k in range(KT):
                    for n, (a, b) in enumerate(((w_hi, x_hi), (w_hi, x_lo), (w_lo, x_hi))):
                        last = mm(o, w(a, k), x(b, k), start=(k == 0 and n == 0), stop=(k == KT - 1 and n == 2))
                return last

            def project(idx, g, what):
                if not (isinstance(idx, int) and idx < 2):
                    pe.wait_ge(rope_mul, idx - 1)
                bank = pj[PJOBS.index(what) % 2]
                col = WSTART[g] + (0 if what in ("K", "E") else (1 + what) * P)
                lo, hi = columns(what)
                split_mm(bank[:, 0:hi - lo], lambda a, k: a[:, k, col:col + P],
                         lambda b, k: b[:, k, lo:hi]).then_inc(proj_done, 1)

            def scores(it, g, j, pair):
                pe.wait_ge(rope_add, it * P_N + g * P_FIRST + 2 * pair + 4)
                if pair == 0:
                    pe.wait_ge(k_ready, it * GROUPS + g + 1)
                if not (isinstance(it, int) and it == 0 and g == 0 and j == 0):
                    pe.wait_ge(exp_done, it * S_N + g * 8 + 2 * j + pair - 1)
                if j == 0 and pair == 0 and g == 0:
                    pe.wait_ge(edge_loaded, it * 16 + 16)
                bank = s_ps[pair][:, 0:2 * KEYS].rearrange("p (u n) -> p u n", u=2)
                for u in range(2):
                    blk = 2 * j + u
                    mm(bank[:, u, :], q_sb[:, g % 2, pair, blk, :],
                       k_sb[:, g % 2, blk, :], start=(u == 0), stop=False)
                if j == 0:
                    last = mm(bank, id_bf[:], edge_sb[:], start=False, stop=True)
                else:
                    last = mm(bank[:, :, FRONT:], id_bf[:], std_sb[:, None, :].broadcast_to([P, 2, 2 * BLK]), start=False, stop=True)
                last.then_inc(s_done, 1)

            def transposes(quad, par):
                pe.wait_ge(front_ready, quad + 1)
                if not (isinstance(quad, int) and quad == 0):
                    pe.wait_ge(pt_ready, quad)
                for n in range(4):
                    nc.tensor.transpose(pt_ps[:, n * P:(n + 1) * P], prob[:, par, n, FRONT:], id_f[:])
                nc.tensor.transpose(pf_ps[:, 0:P], prob_f[:, par, :, :].rearrange("p n k -> p (n k)"), id_f[:]).then_inc(t_done, 1)

            def values(quad, par, g, j):
                pe.wait_ge(pt_ready, quad + 1)
                if not (isinstance(quad, int) and quad == 0):
                    pe.wait_ge(o_ready, quad)
                mm(pv_ps[:, 0:4 * VW], prob_t[:, par, 4 * P:], vf_sb[:, g, :], start=True, stop=False)
                for n in range(4):
                    last = mm(pv_ps[:, n * VW:(n + 1) * VW], prob_t[:, par, n * P:(n + 1) * P],
                              v_sb[:, 2 * j + n % 2, g, :], start=False, stop=(n == 3))
                last.then_inc(pv_done, 1)

            def to_misc(idx):
                if not (isinstance(idx, int) and idx == 0):
                    pe.wait_ge(misc_read, idx)

            def step(name, arg, idx, misc=misc):
                if name not in MISC_JOBS:
                    return
                if misc is misc_bank:
                    to_misc(idx)
                if name in ("V0", "V1"):
                    for n, t in enumerate((0, 1, TILES) if name == "V0" else (2, 3)):
                        at = EXT + t * P if t < TILES else 0
                        o = misc[:, n * 2 * WV:(n + 1) * 2 * WV]
                        mm(o, x_hi[:, 0, at:at + P], wv_sb[:, 0, :], start=True, stop=False)
                        for k in range(KT):
                            mm(o[:, 0:WV], x_lo[:, k, at:at + P], wv_sb[:, k, 0:WV], start=False, stop=False)
                        last = mm(o, x_hi[:, 1, at:at + P], wv_sb[:, 1, :], start=False, stop=True)
                elif name in ("XT0", "XT1", "XTE"):
                    if name == "XT0":
                        pe.wait_ge(x_loaded, arg * 32 + 32)
                    if name == "XTE":
                        for k in range(KT):
                            last = nc.tensor.transpose(misc[:, k * EXT:(k + 1) * EXT], x_in[0:EXT, 0, k * P:(k + 1) * P], id_f[0:EXT, 0:EXT])
                    else:
                        k = int(name[2])
                        for t in range(TILES):
                            last = nc.tensor.transpose(misc[:, t * P:(t + 1) * P], x_in[:, 1 + t, k * P:(k + 1) * P], id_f[:])
                elif name in ("OT0", "OT1"):
                    pe.wait_ge(o_ready, arg * Q_N + Q_N - 2 + 2 * int(name[2]))
                    for u in range(4):
                        last = nc.tensor.transpose(misc[:, u * P:(u + 1) * P], o_sb[:, 4 * int(name[2]) + u, :], id_f[:])
                elif name in ("OP0", "OP1", "G0", "G1"):
                    if name == "OP0":
                        pe.wait_ge(og_ready, 1)
                    w = 0 if name[0] == "O" else 1
                    for t in range(2):
                        last = split_mm(misc[:, t * D:(t + 1) * D], lambda a, k: (e_hi if a is w_hi else e_lo)[:, k, t * P:(t + 1) * P],
                                        lambda b, k: (og_hi if b is x_hi else og_lo)[:, w, k, :])
                elif name in ("X1T0", "X1T1"):
                    a = int(name[3])
                    pe.wait_ge(x1_ready, arg * 2 + a + 1)
                    for k in range(KT):
                        for t in range(2):
                            last = nc.tensor.transpose(misc[:, (2 * k + t) * P:(2 * k + t + 1) * P], x1[:, 2 * a + t, k * P:(k + 1) * P], id_f[:])
                elif name in ("TN", "TT", "TU"):
                    pe.wait_ge(th_rows, {"TN": 1, "TU": 2 + STEPS}.get(name, 2 + arg))
                    rows = th if name == "TU" else tn
                    for k in range(KT):
                        last = nc.tensor.transpose(misc[:, k * BATCH:(k + 1) * BATCH], rows[:, k * P:(k + 1) * P], id_f[0:BATCH, 0:BATCH])
                elif name == "TA":
                    for k in range(KT):
                        last = mm(misc[0:BATCH, 0:D], t_t[:, k, :], agg_w[:, k, :], start=(k == 0), stop=(k == KT - 1))
                elif name == "TH":
                    for m in range(HT):
                        for k in range(KT):
                            last = mm(misc[:, m * BATCH:(m + 1) * BATCH], d1_w[:, k, m * P:(m + 1) * P], t_t[:, k, :], start=(k == 0), stop=(k == KT - 1))
                elif name == "TD":
                    pe.wait_ge(gelu_ready, arg + 1)
                    for m in range(HT):
                        last = mm(misc[0:BATCH, 0:D], hid_g[:, m, :], d2_w[:, m, :], start=(m == 0), stop=(m == HT - 1))
                else:
                    for b in range(2):
                        for k in range(KT):
                            row = t_t[:, k, 2 * int(name[2]) + b:2 * int(name[2]) + b + 1].broadcast_to([P, P])
                            last = mm(misc[:, b * D:(b + 1) * D], row, bc_w[:, k, :], start=(k == 0), stop=(k == KT - 1))
                last.then_inc(misc_done, 1)

            pe.wait_ge(id_loaded, 16)
            for n, name in enumerate(("XT0", "XT1", "XTE")):
                step(name, 0, n, first_banks[n])
            pe.wait_ge(misc_read, N_PREP)
            pe.wait_ge(w_split[0], 1)
            for n, what in enumerate(PJOBS):
                project(n, 0, what)
            pe.wait_ge(c_loaded, 32)
            pe.wait_ge(const_set, 1)

            def body(it, kind):
                st = state_of(it, kind)
                x_read = None
                for q in range(Q_N):
                    g, j = q // 4, q % 4
                    quad = it * Q_N + q
                    for pair, place in ((0, "A"), (1, "B")):
                        scores(it, g, j, pair)
                        if pair == 0 and (kind != "first" or q >= 2):
                            if q == 2:
                                pe.wait_ge(misc_read, st["base"] + 2)
                            values(quad - 2, q % 2, (q - 2) % Q_N // 4, (q - 2) % 4)
                        for name, arg, idx in walk(kind, it, (q, place), st):
                            step(name, arg, idx)
                            if name == "XTE":
                                x_read = idx + 1
                        p = proj_at(g, j, place)
                        if p and not (kind == "last" and g == 3):
                            if p[0] == 18:
                                pe.wait_ge(misc_read, x_read)
                            if kind == "first" and p[1] == "K" and g < GROUPS - 1:
                                pe.wait_ge(w_split[g + 1], 1)
                            project(P_FIRST + it * P_N + p[0], (g + 1) % 4, p[1])
                        if pair == 0 and (kind != "first" or q >= 1):
                            transposes(quad - 1, (q - 1) % 2)
                    for name, arg, idx in walk(kind, it, (q, "C"), st):
                        step(name, arg, idx)

            chunks(pe, body)
            values(NCH * Q_N - 2, 0, 3, 2)
            transposes(NCH * Q_N - 1, 1)
            values(NCH * Q_N - 1, 1, 3, 3)
            for name, arg, idx in tail_steps():
                step(name, arg, idx, tail_bank(name))

        @block.vector
        def _(dve):
            v = nc.vector

            def rotate(idx, what):
                dve.wait_ge(proj_done, idx + 1)
                if not (isinstance(idx, int) and idx < 2):
                    dve.wait_ge(rope_add, idx - 1)
                par = PJOBS.index(what) % 2
                lo, hi = columns(what)
                n, half = hi - lo, P // 2
                v.tensor_tensor(rope_c[:, par, 0:n], pj[par][:, 0:n], rope_sb[:, 0, lo:hi], ALU.mult)
                v.tensor_tensor(rope_s[half:P, par, 0:n], pj[par][0:half, 0:n], rope_sb[0:half, 1, lo:hi], ALU.mult)
                v.tensor_tensor(rope_s[0:half, par, 0:n], pj[par][half:P, 0:n], rope_sb[half:P, 1, lo:hi], ALU.mult).then_inc(rope_mul, 1)

            def row_max(idx, pair, slot):
                dve.wait_ge(s_done, idx + 1)
                v.tensor_reduce(out=neg_max[:, slot, :], in_=s_ps[pair][:, 0:2 * KEYS].rearrange("p (u n) -> p u n", u=2),
                                axis=AX.X, op=ALU.max, negate=True).then_inc(max_done, 1)

            def normalize(quad, par):
                dve.wait_ge(pv_done, quad + 1)
                units = pv_ps[:, 0:4 * VW].rearrange("p (n e) -> p n e", e=VW)
                v.reciprocal(rcp[:, par, :], units[:, :, DV]).then_inc(rcp_done, 1)

            def normalize_out(quad, par, g, j):
                dve.wait_ge(rcp_done, quad + 1)
                units = pv_ps[:, 0:4 * VW].rearrange("p (r u e) -> p r u e", r=2, e=VW)
                dst = o_sb[:, 2 * j:2 * j + 2, g * 2 * DV:(g + 1) * 2 * DV].rearrange("p u (r d) -> p r u d", r=2)
                v.tensor_tensor(dst, units[:, :, :, 0:DV], rcp[:, par, :].rearrange("p (r u) -> p r u", r=2)[:, :, :, None].broadcast_to([P, 2, 2, DV]),
                                ALU.mult).then_inc(o_ready, 1)

            def statistics(src, a, st, m, link, n, done):
                for t in (2 * a, 2 * a + 1):
                    last = v.bn_stats(st[:, t, :], src[:, t, :])
                last.then_inc(link, 1)
                dve.wait_ge(link, n + 1)
                v.memset(carry[:], 0.0)
                for t in (2 * a, 2 * a + 1):
                    last = v.bn_aggr(m[:, t, :], st[:, t, :])
                last.then_inc(done, 1)

            def th_norm(rows, gamma, n):
                v.bn_stats(tst[:], rows).then_inc(th_link, 1)
                chain()
                v.bn_aggr(tmv[:], tst[:]).then_inc(th_mv, 1)
                dve.wait_ge(th_mv, n + 1)
                v.scalar_tensor_tensor(out=tn, in0=rows, scalar=tmv[:, 0:1], in1=gamma, op0=ALU.subtract, op1=ALU.mult).then_inc(th_link, 1)

            links = [0]

            def chain():
                links[0] += 1
                dve.wait_ge(th_link, links[0])

            def step(name, arg, idx, misc=misc):
                if name in MISC_JOBS:
                    dve.wait_ge(misc_done, idx + 1)
                if name in ("V0", "V1"):
                    a = int(name[1])
                    if a == 0:
                        if not (isinstance(arg, int) and arg == 0):
                            dve.wait_ge(pv_done, arg * Q_N)
                        else:
                            dve.wait_ge(const_set, 1)
                    half = P // 2

                    def values_to(dst, rows, tiles):
                        return v.tensor_tensor(dst, v_ps[rows, tiles, 0], v_low[rows, tiles, :, :], ALU.add)

                    dve.wait_ge(v_low_ready, arg * 2 + a + 1)
                    values_to(v_sb[:, 4 * a + 1:4 * a + 4:2, :, 0:DV], slice(0, P), slice(0, 2))
                    values_to(v_sb[half:P, 4 * a:4 * a + 4:2, :, 0:DV], slice(0, half), slice(0, 2))
                    if a == 0:
                        values_to(v_sb[0:half, 2:5:2, :, 0:DV], slice(half, P), slice(0, 2))
                        values_to(v_sb[0:half, 0, :, 0:DV], slice(0, half), 2)
                        for n in range(4):
                            last = values_to(vf_sb[n * FRONT:(n + 1) * FRONT, :, n * VW:n * VW + DV], slice(BLK, EXT), 2)
                    else:
                        last = values_to(v_sb[0:half, 6, :, 0:DV], slice(half, P), 0)
                    last.then_inc(misc_read, 1)
                elif name in ("XT0", "XT1", "XTE"):
                    dve.wait_ge(xhi_ready, arg * 3 + ("XT0", "XT1", "XTE").index(name) + 1)
                    if name == "XTE":
                        dst, hi, src = x_lo[:, :, 0:EXT], x_hi[:, :, 0:EXT], misc[:, 0:KT * EXT].rearrange("p (k n) -> p k n", k=KT)
                    else:
                        k = int(name[2])
                        dst, hi, src = x_lo[:, k, EXT:], x_hi[:, k, EXT:], misc[:, :]
                    v.tensor_tensor(dst, src, hi.bitcast(f32), ALU.subtract).then_inc(misc_read, 1)
                elif name in ("OT0", "OT1", "X1T0", "X1T1"):
                    a = int(name[-1])
                    dve.wait_ge(ehi_ready, arg * 4 + a + (1 if name[0] == "O" else 3))
                    lo, hi, src = e_lo[:, :, :], e_hi[:, :, :].bitcast(f32), misc[:, :].rearrange("p (k n) -> p k n", k=KT)
                    if name[0] == "O":
                        src = misc[:, :].rearrange("p (u h q) -> p h u q", u=4, h=2)
                        lo, hi = (x.rearrange("p h (u q) -> p h u q", u=4) for x in (lo, hi))
                    v.tensor_tensor(lo, src, hi, ALU.subtract).then_inc(misc_read, 1)
                elif name in ("OP0", "OP1"):
                    a = int(name[2])
                    if a == 0:
                        dve.wait_ge(res_loaded, arg * 16 + 16)
                    v.tensor_tensor(y[:, 2 * a:2 * a + 2, :], misc[:, :].rearrange("p (t d) -> p t d", t=2), y[:, 2 * a:2 * a + 2, :], ALU.add).then_inc(misc_read, 1)
                    last_res[a] = idx + 1
                elif name in ("BN0", "BN1"):
                    a = int(name[2])
                    dve.wait_ge(misc_read, last_res[a])
                    statistics(y, a, stats, mv, bn_done, arg * 2 + a, mv_ready)
                elif name in ("G0", "G1"):
                    a = int(name[1])
                    if a == 0:
                        free_z(arg)
                    v.tensor_tensor(z[:, 2 * a:2 * a + 2, :], misc[:, :].rearrange("p (t d) -> p t d", t=2),
                                    gate_b[:, None, :].broadcast_to([P, 2, D]), ALU.add).then_inc(misc_read, 1)
                elif name[0] == "F":
                    final(name, *arg)
                elif name[0] == "T":
                    thought(name, arg, idx)

            last_res = [0, 0]
            state = {"kind": None}

            def free_z(arg):
                if isinstance(arg, int) and arg == 0:
                    return
                dve.wait_ge(tanh_ready, arg * 2)
                if state["kind"] not in ("store", "thought"):
                    dve.wait_ge(f_gated, (arg - NSTORE) * 4 + 1)

            def final(name, src, n, fi):
                xs, ts, b = sources(src, n)
                if name[1] not in "ABGD":
                    return
                a = int(name[2])
                tiles = slice(2 * a, 2 * a + 2)
                if name[1] == "A":
                    dve.wait_ge(tanh_ready, n * 2 + (a + 1 if src == "E" else 2))
                    dve.wait_ge(misc_read, thought_over)
                    v.scalar_tensor_tensor(out=f1[:, tiles, :], in0=ts[:, tiles, :], scalar=1.0, in1=b.broadcast_to([P, 2, D]), op0=ALU.add, op1=ALU.mult).then_inc(f_gated, 1)
                    if state["kind"] == "tail" and src == "E":
                        dve.wait_ge(f_gated, 2 * fi + a + 2)
                        v.tensor_tensor(f1[:, tiles, :], f1[:, tiles, :], xs[:, tiles, :], ALU.add).then_inc(f_sum, 1)
                elif name[1] == "G":
                    dve.wait_ge(f_norm, 2 * fi + a + 1)
                    v.tensor_tensor(f2[:, tiles, :], f2[:, tiles, :], out_gamma[:, None, :].broadcast_to([P, 2, D]), ALU.mult).then_inc(f_scaled, 1)
                    if state["kind"] == "tail" and src == "E":
                        dve.wait_ge(f_beta, 2 * fi + a + 1)
                        dve.wait_ge(f_scaled, 2 * fi + a + 1)
                        v.tensor_tensor(f2[:, tiles, :], f2[:, tiles, :], f_x[:, tiles, :], ALU.add).then_inc(f_added, 1)
                elif name[1] == "B":
                    dve.wait_ge(f_sum, 2 * fi + a + 1)
                    statistics(f1, a, fstats, fmv, f_bn, 4 * fi + a, f_mv)
                else:
                    dve.wait_ge(f_added, 2 * fi + a + 2)
                    statistics(f2, a, fstats, fmv, f_bn, 4 * fi + 2 + a, f_mv)

            def thought(name, n, idx):
                rows = misc[0:BATCH, 0:D]
                if name == "TX":
                    dve.wait_ge(ffn_loaded, 144)
                    v.tensor_scalar(out=bc_b, in0=bc_b, scalar1=0.5, scalar2=None, op0=ALU.mult).then_inc(th_link, 1)
                    chain()
                    dve.wait_ge(tail_x, 32)
                    th_norm(last_x, in_gamma, 0)
                elif name == "TM":
                    chain()
                    dve.wait_ge(th_rstd, n + 1)
                    v.scalar_tensor_tensor(out=tn, in0=tn, scalar=trs[:, 1:2], in1=in_beta if n == 0 else pn_beta, op0=ALU.mult, op1=ALU.add).then_inc(th_rows, 1)
                elif name in ("TN", "TT", "TU"):
                    v.tensor_copy(t_t[:, :, :], misc[:, 0:KT * BATCH].rearrange("p (k b) -> p k b", k=KT)).then_inc(misc_read, 1)
                elif name == "TA":
                    v.tensor_tensor(th, rows, agg_b, ALU.add).then_inc(misc_read, 1)
                    dve.wait_ge(misc_read, idx + 1)
                    th_norm(th, pn_gamma, 1)
                elif name == "TH":
                    v.tensor_tensor(hid[:], misc[:, 0:HT * BATCH].rearrange("p (m b) -> p m b", m=HT), d1_b[:, :, None].broadcast_to([P, HT, BATCH]), ALU.add).then_inc(misc_read, 1)
                elif name == "TD":
                    v.tensor_tensor(tn, rows, d2_b, ALU.add).then_inc(misc_read, 1)
                    dve.wait_ge(misc_read, idx + 1)
                    last = v.tensor_tensor(th, th, tn, ALU.add)
                    if n < STEPS - 1:
                        last.then_inc(th_link, 1)
                        chain()
                        th_norm(th, pn_gamma, 2 + n)
                    else:
                        last.then_inc(th_rows, 1)
                else:
                    a = int(name[2])
                    v.scalar_tensor_tensor(out=bc_sb[:, 2 * a:2 * a + 2, :], in0=misc[:, :].rearrange("p (b d) -> p b d", b=2), scalar=0.5,
                                           in1=bc_b[:, None, :].broadcast_to([P, 2, D]), op0=ALU.mult, op1=ALU.add).then_inc(misc_read, 1)

            v.memset(vf_sb[:], 0.0).then_inc(const_step, 1)
            dve.wait_ge(const_step, 1)
            for n in range(4):
                v.memset(vf_sb[n * FRONT:(n + 1) * FRONT, :, n * VW + DV:(n + 1) * VW], 1.0)
            v.memset(eps1[:], EPS1)
            v.memset(eps2[:], EPS2)
            v.memset(frstd[0][:], 0.0).then_inc(f_gated, 1)
            v.memset(half_pow[:], -0.5).then_inc(f_added, 1)
            v.memset(minus_one[:], -1.0).then_inc(f_out, 1)
            v.memset(carry[:], 0.0).then_inc(stored, 16)
            v.memset(v_sb[:, :, :, DV:VW], 1.0).then_inc(const_set, 1)

            def low_part(g):
                dve.wait_ge(hi_split, g + 1)
                cols = slice(WSTART[g], WEND[g])
                if g == 0:
                    v.tensor_tensor(wv_sb[:, :, WV:], stage_w[:, :, WV0:WV0 + WV], wv_sb[:, :, 0:WV].bitcast(f32), ALU.subtract)
                v.tensor_tensor(w_lo[:, :, cols], stage_w[:, :, cols], w_hi[:, :, cols].bitcast(f32), ALU.subtract).then_inc(w_split[g], 1)

            for n, name in enumerate(("XT0", "XT1", "XTE")):
                step(name, 0, n, first_banks[n])
            low_part(0)
            dve.wait_ge(rope_loaded, 16)
            for n, what in enumerate(PJOBS):
                rotate(n, what)
                if what == "E":
                    low_part(1)

            def body(it, kind):
                state["kind"] = kind
                st = state_of(it, kind)
                for q in range(Q_N):
                    g, j = q // 4, q % 4
                    quad = it * Q_N + q
                    for pair, place in ((0, "A"), (1, "B")):
                        row_max(it * S_N + q * 2 + pair, pair, (q * 2 + pair) % 4)
                        if pair == 0 and (kind != "first" or q >= 2):
                            normalize(quad - 2, q % 2)
                            if q in (2, 4) and kind != "first":
                                dve.wait_ge(misc_done, st["base"] + 1 + q)
                            normalize_out(quad - 2, q % 2, (q - 2) % Q_N // 4, (q - 2) % 4)
                        for name, arg, idx in walk(kind, it, (q, place), st):
                            step(name, arg, idx)
                        p = proj_at(g, j, place)
                        if p and not (kind == "last" and g == 3):
                            if p[0] == 18:
                                dve.wait_ge(rope_loaded, it * 16 + 32)
                            rotate(P_FIRST + it * P_N + p[0], p[1])
                    for name, arg, idx in walk(kind, it, (q, "C"), st):
                        step(name, arg, idx)

            chunks(dve, body)
            state["kind"] = "tail"
            for n in (2, 1):
                normalize(NCH * Q_N - n, n % 2)
                normalize_out(NCH * Q_N - n, n % 2, 3, 4 - n)
            for name, arg, idx in tail_steps():
                step(name, arg, idx, tail_bank(name))

        @block.scalar
        def _(act):
            sc = nc.scalar

            def exps(quad, q, pair):
                idx = 2 * quad + pair
                act.wait_ge(max_done, idx + 1)
                if not (isinstance(quad, int) and quad < 2):
                    act.wait_ge(t_done, quad - 1)
                for u in range(2):
                    last = sc.activation(prob[:, q % 2, 2 * pair + u, :], s_ps[pair][:, u * KEYS:(u + 1) * KEYS], ACT.Exp,
                                         bias=neg_max[:, (q * 2 + pair) % 4, u:u + 1], scale=1.0)
                last.then_inc(exp_done, 1)

            def gather_front(quad, q):
                act.wait_ge(exp_done, 2 * quad + 2)
                sc.copy(prob_f[:, q % 2, :, :], prob[:, q % 2, :, 0:FRONT]).then_inc(front_ready, 1)

            def copy_transposed(quad, par):
                act.wait_ge(t_done, quad + 1)
                if not (isinstance(quad, int) and quad < 2):
                    act.wait_ge(pv_done, quad - 1)
                sc.copy(prob_t[:, par, 0:4 * P], pt_ps[:, :])
                sc.copy(prob_t[:, par, 4 * P:], pf_ps[:, 0:P]).then_inc(pt_ready, 1)

            def spread_keys(stage, par):
                act.wait_ge(rope_add, stage * P_FIRST + 2)
                sc.copy(k_sb[:, par, 0, FRONT:FRONT + BLK], k_ext[:, 0:BLK])
                sc.copy(k_sb[:, par, 1:, FRONT:FRONT + BLK], k_sb[:, par, 0:NBLK - 1, FRONT + BLK:])
                sc.copy(k_sb[:, par, :, 0:FRONT], k_ext[:, None, BLK:].broadcast_to([P, NBLK, FRONT])).then_inc(k_ready, 1)

            def apply_norm(dst, src, a, work, done):
                for t in (2 * a, 2 * a + 1):
                    last = sc.activation(dst[:, t, :], src[:, t, :], ACT.Identity, bias=work[:, 2, t:t + 1], scale=work[:, 1, t:t + 1])
                last.then_inc(done, 1)

            def free_x1(arg, kind):
                if kind in ("store", "thought"):
                    act.wait_ge(x1_stored, arg * 16)
                else:
                    act.wait_ge(x1_stored, NSTORE * 16)
                    act.wait_ge(f_added, (arg - NSTORE) * 4 + 1)

            def step(name, arg, idx, kind, misc=misc):
                if name in PE_FED:
                    act.wait_ge(misc_done, idx + 1)
                if name in ("V0", "V1"):
                    n = 3 - int(name[1])
                    sc.copy(v_low[:, 0:n, :, :], v_ps[:, 0:n, 1]).then_inc(v_low_ready, 1)
                if name in ("XT0", "XT1", "XTE"):
                    if name == "XT0" and not (isinstance(arg, int) and arg == 0):
                        act.wait_ge(proj_done, arg * P_N)
                    if name == "XTE":
                        sc.copy(x_hi[:, :, 0:EXT], misc[:, 0:KT * EXT].rearrange("p (k n) -> p k n", k=KT)).then_inc(xhi_ready, 1)
                    else:
                        sc.copy(x_hi[:, int(name[2]), EXT:], misc[:, :]).then_inc(xhi_ready, 1)
                elif name in ("OT0", "OT1"):
                    dst = e_hi[:, :, :].rearrange("p h (u q) -> p h u q", u=4)
                    sc.copy(dst, misc[:, :].rearrange("p (u h q) -> p h u q", u=4, h=2)).then_inc(ehi_ready, 1)
                elif name in ("X1T0", "X1T1"):
                    sc.copy(e_hi[:, :, :], misc[:, :].rearrange("p (k n) -> p k n", k=KT)).then_inc(ehi_ready, 1)
                elif name == "WH":
                    act.wait_ge(ffn_loaded, 144)
                    sc.copy(og_hi[:], og_w).then_inc(og_split, 1)
                elif name in ("NM0", "NM1"):
                    a = int(name[2])
                    act.wait_ge(rstd_ready, arg * 2 + a + 1)
                    if a == 0 and not (isinstance(arg, int) and arg == 0):
                        free_x1(arg, kind)
                    apply_norm(x1, y, a, rstd, x1_ready)
                elif name in ("G0", "G1"):
                    act.wait_ge(misc_read, idx + 1)
                    a = int(name[1])
                    src = z[:, 2 * a:2 * a + 2, :].rearrange("p t d -> p (t d)")
                    dst = src
                    if kind in ("store", "thought"):
                        dst = store[:, 1, bass.ds(arg, 1), a * 2 * D:(a + 1) * 2 * D].rearrange("p a d -> p (a d)")
                    sc.activation(dst, src, ACT.Tanh, scale=0.5).then_inc(tanh_ready, 1)
                elif name == "TH":
                    act.wait_ge(misc_read, idx + 1)
                    sc.activation(hid_g[:], hid[:], ACT.Gelu).then_inc(gelu_ready, 1)
                elif name in ("FC0", "FC1"):
                    a = int(name[2])
                    act.wait_ge(f_rstd, 4 * arg[2] + a + 1)
                    act.wait_ge(f_out, 2 * arg[2] + 1)
                    apply_norm(f2, f1, a, frstd[0], f_norm)
                elif name in ("FE0", "FE1"):
                    a = int(name[2])
                    fi = arg[2]
                    act.wait_ge(f_rstd, 4 * fi + a + 3)
                    if a == 0:
                        act.wait_ge(stored, fi * 32 + 16)
                    apply_norm(f_o, f2, a, frstd[1], f_out)

            def high_part(g):
                act.wait_ge(w_loaded[g], 16)
                cols = slice(WSTART[g], WEND[g])
                if g == 0:
                    sc.copy(wv_sb[:, :, 0:WV], stage_w[:, :, WV0:WV0 + WV])
                sc.copy(w_hi[:, :, cols], stage_w[:, :, cols]).then_inc(hi_split, 1)

            for n, name in enumerate(("XT0", "XT1", "XTE")):
                step(name, 0, n, "first", first_banks[n])
            for g in range(GROUPS):
                high_part(g)
            spread_keys(0, 0)

            def body(it, kind):
                st = state_of(it, kind)
                for q in range(Q_N):
                    g, j = q // 4, q % 4
                    quad = it * Q_N + q
                    for pair, place in ((0, "A"), (1, "B")):
                        steps = list(walk(kind, it, (q, place), st))
                        early = [pair == 1 and name in PE_FED for name, _, _ in steps]
                        for (name, arg, idx), first in zip(steps, early):
                            if first:
                                step(name, arg, idx, kind)
                        exps(quad, q, pair)
                        if pair == 1:
                            gather_front(quad, q)
                        for (name, arg, idx), first in zip(steps, early):
                            if not first:
                                step(name, arg, idx, kind)
                        if pair == 0 and not (kind == "first" and q == 0):
                            copy_transposed(quad - 1, (q - 1) % 2)
                        if place == "A" and j > 0:
                            p = proj_at(g, j - 1, "B")
                            if p and p[1] == "E" and not (kind == "last" and g == 3):
                                spread_keys(it * GROUPS + g + 1, (g + 1) % 2)
                    for name, arg, idx in walk(kind, it, (q, "C"), st):
                        step(name, arg, idx, kind)

            chunks(act, body)
            copy_transposed(NCH * Q_N - 1, 1)
            for name, arg, idx in tail_steps():
                step(name, arg, idx, "tail", tail_bank(name))

        @block.gpsimd
        def _(pool):
            gp = nc.gpsimd

            def add(stage, par, what):
                k = PJOBS.index(what)
                pool.wait_ge(rope_mul, stage * P_FIRST + k + 1)
                lo, hi = columns(what)
                c, s = rope_c[:, k % 2, 0:hi - lo], rope_s[:, k % 2, 0:hi - lo]
                if what == "K":
                    if not (isinstance(stage, int) and stage < 2):
                        pool.wait_ge(s_done, (stage - 1) * 8)
                    if not (isinstance(stage, int) and stage == 0):
                        pool.wait_ge(k_ready, stage)
                    gp.tensor_tensor(k_ext[:, :], c[:, 0:EXT], s[:, 0:EXT], ALU.add)
                    c, s = c[:, EXT:], s[:, EXT:]
                    dst = k_sb[:, par, 0:3, FRONT + BLK:]
                elif what == "E":
                    dst = k_sb[:, par, 3:, FRONT + BLK:]
                else:
                    dst = q_sb[:, par, what // 2, :, what % 2 * BLK:(what % 2 + 1) * BLK]
                c, s = (a.rearrange("p (u n) -> p u n", n=BLK) for a in (c, s))
                gp.tensor_tensor(dst, c, s, ALU.add).then_inc(rope_add, 1)

            def inverse_root(m, a, work, eps, ve, n, done):
                h = slice(2 * a, 2 * a + 2)
                gp.tensor_tensor(work[:, 0, h], m[:, h, 1], eps[:, h], ALU.add).then_inc(ve, 1)
                gp.tensor_tensor(work[:, 2, h], m[:, h, 0], minus_one[:, h], ALU.mult).then_inc(ve, 1)
                pool.wait_ge(ve, 3 * n + 2)
                gp.tensor_tensor(work[:, 1, h], work[:, 0, h], half_pow[:, h], ALU.pow).then_inc(ve, 1)
                pool.wait_ge(ve, 3 * n + 3)
                gp.tensor_tensor(work[:, 2, h], work[:, 2, h], work[:, 1, h], ALU.mult).then_inc(done, 1)

            def th_inverse_root(n):
                pool.wait_ge(th_mv, n + 1)
                gp.tensor_tensor(trs[:, 0:1], tmv[:, 1:2], eps2[0:BATCH, 0:1], ALU.add).then_inc(th_ve, 1)
                pool.wait_ge(th_ve, n + 1)
                gp.tensor_tensor(trs[:, 1:2], trs[:, 0:1], half_pow[0:BATCH, 0:1], ALU.pow).then_inc(th_rstd, 1)

            def step(name, arg, idx):
                if name == "WL":
                    pool.wait_ge(og_split, 1)
                    gp.tensor_tensor(og_lo[:], og_w, og_hi[:].bitcast(f32), ALU.subtract).then_inc(og_ready, 1)
                elif name in ("BN0", "BN1"):
                    a = int(name[2])
                    pool.wait_ge(mv_ready, arg * 2 + a + 1)
                    inverse_root(mv, a, rstd, eps1, ve_ready, arg * 2 + a, rstd_ready)
                elif name in ("TX", "TA") or name == "TD" and arg < STEPS - 1:
                    th_inverse_root({"TX": 0, "TA": 1}.get(name, 2 + arg))
                elif name[0] == "F":
                    src, n, fi = arg
                    xs, _, _ = sources(src, n)
                    a = int(name[2])
                    if isinstance(fi, int) and fi == NCH - 1 and name[1] in "AG":
                        return
                    tiles = slice(2 * a, 2 * a + 2)
                    if name[1] == "A":
                        pool.wait_ge(f_gated, 2 * fi + a + 2)
                        if src == "S":
                            pool.wait_ge(x1_stored, n * 16 + 16)
                        gp.tensor_tensor(f1[:, tiles, :], f1[:, tiles, :], xs[:, tiles, :], ALU.add).then_inc(f_sum, 1)
                    elif name[1] == "X":
                        if src == "E":
                            pool.wait_ge(x1_ready, n * 2 + a + 1)
                        gp.tensor_tensor(f_x[:, tiles, :], xs[:, tiles, :], out_beta[:, None, :].broadcast_to([P, 2, D]), ALU.add).then_inc(f_beta, 1)
                    elif name[1] in "BD":
                        first = name[1] == "B"
                        k = 4 * fi + a + (0 if first else 2)
                        pool.wait_ge(f_mv, k + 1)
                        inverse_root(fmv, a, frstd[0 if first else 1], eps2 if first else eps1, f_ve, k, f_rstd)
                    elif name[1] == "G":
                        pool.wait_ge(f_beta, 2 * fi + a + 1)
                        pool.wait_ge(f_scaled, 2 * fi + a + 1)
                        gp.tensor_tensor(f2[:, tiles, :], f2[:, tiles, :], f_x[:, tiles, :], ALU.add).then_inc(f_added, 1)

            pool.wait_ge(const_set, 1)
            for what in PJOBS:
                add(0, 0, what)
            for g in range(2, GROUPS):
                pool.wait_ge(hi_split, g + 1)
                cols = slice(WSTART[g], WEND[g])
                gp.tensor_tensor(w_lo[:, :, cols], stage_w[:, :, cols], w_hi[:, :, cols].bitcast(f32), ALU.subtract).then_inc(w_split[g], 1)

            def body(it, kind):
                st = state_of(it, kind)
                for q in range(Q_N):
                    g, j = q // 4, q % 4
                    for place in "ABC":
                        for name, arg, idx in walk(kind, it, (q, place), st):
                            step(name, arg, idx)
                        p = proj_at(g, j, place)
                        if p and not (kind == "last" and g == 3):
                            add(it * GROUPS + g + 1, (g + 1) % 2, p[1])

            chunks(pool, body)
            for name, arg, idx in tail_steps():
                step(name, arg, idx)


def kernel(**inputs):
    import numpy as np
    import concourse.bacc as bacc
    from concourse.bass_utils import run_bass_kernel_spmd

    a = {k: np.asarray(v) for k, v in inputs.items()}
    import ml_dtypes
    bf = ml_dtypes.bfloat16
    f = np.float32

    def split_rows(w, tiles):
        return np.ascontiguousarray(w.reshape(tiles, P, -1).transpose(1, 0, 2))

    x = a["L0_attn_x"]
    steps = []
    for it in range(NCH):
        b, c = it % BATCH, 1 - it // BATCH
        prev = max(c * CHUNK - BLK, 0)
        steps.append(np.concatenate([x[b, prev:prev + BLK], x[b, :FRONT], x[b, c * CHUNK:(c + 1) * CHUNK]]))
    order = np.concatenate([np.arange(0, P, 2), np.arange(1, P, 2)])
    wq = a["L0_attn_wq"].reshape(D, HEADS, P)[:, :, order].reshape(D, HEADS * P)
    wk = a["L0_attn_wk"].reshape(D, GROUPS, P)[:, :, order].reshape(D, GROUPS * P)
    parts = []
    for g in range(GROUPS):
        parts += [wk[:, g * P:(g + 1) * P], wq[:, g * REP * P:(g + 1) * REP * P]]
        if g == 0:
            parts.append(a["L0_attn_wv"])
    w_all = split_rows(np.concatenate(parts, axis=1), KT)
    wo_t = np.ascontiguousarray(a["L0_attn_wo"].reshape(HEADS // 2, 2, DV, D).transpose(0, 2, 1, 3).reshape(P, 2, D))
    inv = (1.0 / 10000.0 ** (np.arange(0, P, 2)[:P // 2].astype(f) / P))
    ang = np.outer(np.arange(SEQ, dtype=f), inv.astype(f))
    cos, sin = np.cos(ang).T.astype(np.float64), np.sin(ang).T.astype(np.float64)
    scale = float(P) ** -0.25
    rope = np.empty((2, P, 2, XW), f)
    for half in range(2):
        c = 1 - half
        prev = max(c * CHUNK - BLK, 0)
        pos = np.concatenate([np.arange(prev, prev + BLK), np.arange(FRONT), np.arange(c * CHUNK, (c + 1) * CHUNK)])
        rope[half, :, 0] = np.concatenate([cos[:, pos], cos[:, pos]]) * scale
        rope[half, :, 1] = np.concatenate([sin[:, pos], -sin[:, pos]]) * scale
    NEG = -1e30
    i, k = np.arange(BLK)[:, None], np.arange(2 * BLK)[None, :]
    std = np.where((k > i) & (k <= i + BLK), 0.0, NEG)
    edge = np.zeros((2, BLK, 2, KEYS))
    edge[:, :, :, FRONT:] = std[:, None, :]
    edge[1, :, 0, :FRONT + BLK] = NEG
    edge[1, :, 1, :FRONT] = np.where(np.arange(FRONT)[None, :] <= i, 0.0, NEG)
    std2, edge2 = np.concatenate([std, std]).astype(bf), np.concatenate([edge, edge], axis=1).astype(bf)
    vec = lambda names, n: np.ascontiguousarray(np.broadcast_to(np.stack([a["L0_ffn_" + x] for x in names]), (n, len(names), D)))
    arrays = {
        "x_steps": np.stack(steps), "w_all": w_all, "wo_t": wo_t, "gate_t": split_rows(a["L0_ffn_gate_w"], KT),
        "agg_t": split_rows(a["L0_ffn_agg_w"], KT), "bc_t": split_rows(a["L0_ffn_bc_w"], KT),
        "d1_t": split_rows(a["L0_ffn_d1_w"], KT), "d2_t": split_rows(a["L0_ffn_d2_w"], HT),
        "d1b_t": np.ascontiguousarray(a["L0_ffn_d1_b"].reshape(HT, P).T),
        "vec128": vec(["gate_b", "out_gamma", "out_beta", "bc_b"], P),
        "vec4": vec(["in_gamma", "in_beta", "agg_b", "pn_gamma", "pn_beta", "d2_b"], BATCH),
        "rope": rope, "mask_std": std2, "mask_edge": edge2, "ident_bf": np.eye(P).astype(bf), "ident_f": np.eye(P, dtype=f),
    }
    nc = bacc.Bacc("TRN2", target_bir_lowering=False, num_devices=1)
    args = [nc.dram_tensor(n, v.shape, mybir.dt.from_np(v.dtype), kind="ExternalInput").ap() for n, v in arrays.items()]
    out = nc.dram_tensor("out", (NCH, CHUNK, D), mybir.dt.float32, kind="ExternalOutput").ap()
    build(nc, *args, out)
    r = run_bass_kernel_spmd(nc, [arrays], core_ids=[0])
    got = r.results[0]["out"]
    return np.ascontiguousarray(got.reshape(2, BATCH, CHUNK, D)[::-1].transpose(1, 0, 2, 3).reshape(BATCH, SEQ, D))
```
